# Optimizing a Trainium2 kernel written in Bass

```python
import numpy as np
import jax
import jax.numpy as jnp

def _softmax(x, axis=-1):
    return jax.nn.softmax(x, axis=axis)

def _gelu(x):
    return jax.nn.gelu(x, approximate=True)

def _silu(x):
    return jax.nn.silu(x)

def _sigmoid(x):
    return jax.nn.sigmoid(x)

def _layernorm(x, axis=-1, eps=1e-05):
    m = jnp.mean(x, axis=axis, keepdims=True)
    v = jnp.var(x, axis=axis, keepdims=True)
    return (x - m) / jnp.sqrt(v + eps)

def _scatter_add(tgt, idx, src, axis=0):
    return tgt.at[idx].add(src)

def _segment_sum(src, seg, n):
    return jax.ops.segment_sum(src, seg, n)
kernel_name = 'mk_adj_resnorm_d1_adj_r2_5933f7'

def setup_inputs(seed: int=0):
    np.random.seed(seed)
    _w = jnp.asarray

    def _rec_inputs():
        import jax
        import jax.numpy as jnp
        _gk = jax.random.key(seed)
        x = -0.0001538 + 1 * jax.random.normal(jax.random.fold_in(_gk, 1), (8, 1024, 384), jnp.float32)
        _a = jax.random.bernoulli(jax.random.fold_in(_gk, 2), 0.0078125, (8, 1024, 1024))
        _a = jnp.logical_or(_a, jnp.eye(1024, dtype=bool))
        adj = _a
        return (x, adj)
    x, adj = _rec_inputs()

    def _L0_gnn_setup():
        import jax, jax.numpy as jnp
        import numpy as np
        B, S, H = (4, 1024, 384)
        NUM_HEADS = 6
        HEAD_SIZE = H // NUM_HEADS
        NEG = -9000000000000000.0

        def _heads(x):
            b, s, _ = x.shape
            return x.reshape(b, s, NUM_HEADS, HEAD_SIZE).transpose(0, 2, 1, 3)
        key = jax.random.key(seed)
        ks = jax.random.split(key, 10)
        seq_inputs = jax.random.normal(ks[0], (B, S, H), dtype=jnp.float32)
        gm = jax.random.randint(ks[1], (B, S, S), 0, 2) > 0
        graph_mask = gm | jnp.eye(S, dtype=bool)[None]
        sc = 1.0 / np.sqrt(H)
        Wq = jax.random.normal(ks[2], (H, H), dtype=jnp.float32) * sc
        bq = jnp.zeros((H,), dtype=jnp.float32)
        Wk = jax.random.normal(ks[3], (H, H), dtype=jnp.float32) * sc
        bk = jnp.zeros((H,), dtype=jnp.float32)
        Wv = jax.random.normal(ks[4], (H, H), dtype=jnp.float32) * sc
        bv = jnp.zeros((H,), dtype=jnp.float32)
        Wf = jax.random.normal(ks[5], (H, H), dtype=jnp.float32) * sc
        bf = jnp.zeros((H,), dtype=jnp.float32)
        return {'seq_inputs': seq_inputs, 'Wq': Wq, 'bq': bq, 'Wk': Wk, 'bk': bk, 'Wv': Wv, 'bv': bv, 'Wf': Wf, 'bf': bf, 'graph_mask': graph_mask}
    _L0_gnn_all = _L0_gnn_setup()
    _L0_gnn_in = {k: v for k, v in _L0_gnn_all.items() if k in ('Wq', 'bq', 'Wk', 'bk', 'Wv', 'bv', 'Wf', 'bf')}
    del _L0_gnn_all
    return {'x': x, 'adj': adj, 'L0_gnn_Wq': _L0_gnn_in['Wq'], 'L0_gnn_bq': _L0_gnn_in['bq'], 'L0_gnn_Wk': _L0_gnn_in['Wk'], 'L0_gnn_bk': _L0_gnn_in['bk'], 'L0_gnn_Wv': _L0_gnn_in['Wv'], 'L0_gnn_bv': _L0_gnn_in['bv'], 'L0_gnn_Wf': _L0_gnn_in['Wf'], 'L0_gnn_bf': _L0_gnn_in['bf']}

def reference(x, adj, L0_gnn_Wq, L0_gnn_bq, L0_gnn_Wk, L0_gnn_bk, L0_gnn_Wv, L0_gnn_bv, L0_gnn_Wf, L0_gnn_bf):
    import jax
    import jax.numpy as jnp

    def _L0_gnn_ref(seq_inputs, Wq, bq, Wk, bk, Wv, bv, Wf, bf, graph_mask):
        import jax, jax.numpy as jnp
        import numpy as np
        B, S, H = (4, 1024, 384)
        NUM_HEADS = 6
        HEAD_SIZE = H // NUM_HEADS
        NEG = -9000000000000000.0

        def _heads(x):
            b, s, _ = x.shape
            return x.reshape(b, s, NUM_HEADS, HEAD_SIZE).transpose(0, 2, 1, 3)
        q = _heads(seq_inputs @ Wq + bq)
        k = _heads(seq_inputs @ Wk + bk)
        v = _heads(seq_inputs @ Wv + bv)
        scores = jnp.einsum('bhqd,bhkd->bhqk', q, k) / np.sqrt(HEAD_SIZE)
        bias = jnp.where(graph_mask, 0.0, NEG)[:, None]
        probs = jax.nn.softmax(scores + bias, axis=-1)
        ctx = jnp.einsum('bhqk,bhkd->bhqd', probs, v)
        ctx = ctx.transpose(0, 2, 1, 3).reshape(seq_inputs.shape[0], seq_inputs.shape[1], H)
        return ctx @ Wf + bf
    x = _layernorm(x + _L0_gnn_ref(x, L0_gnn_Wq, L0_gnn_bq, L0_gnn_Wk, L0_gnn_bk, L0_gnn_Wv, L0_gnn_bv, L0_gnn_Wf, L0_gnn_bf, adj), axis=-1)
    return x

_drawn_inputs = setup_inputs


def setup_inputs(seed=0):
    import zlib

    import numpy as np

    out = dict(_drawn_inputs(seed))
    spreads = {'L0_gnn_bq': (0.0, 0.1),
     'L0_gnn_bk': (0.0, 0.1),
     'L0_gnn_bv': (0.0, 0.1),
     'L0_gnn_bf': (0.0, 0.1)}
    factors = {}
    for name, (base, spread) in spreads.items():
        noise = np.random.default_rng([zlib.crc32(name.encode()), seed]).standard_normal(out[name].shape)
        drawn = base * np.exp(spread * noise) if base else spread * noise
        out[name] = jnp.asarray(drawn.astype(out[name].dtype))
    for name, factor in factors.items():
        out[name] = (out[name] * factor).astype(out[name].dtype)
    return out
```

```python
from contextlib import ExitStack

import concourse.bass as bass
from concourse import mybir

F32 = mybir.dt.float32
F32R = mybir.dt.float32r
U8 = mybir.dt.uint8
ALU = mybir.AluOpType
ACT = mybir.ActivationFunctionType

P = 128
NEG = 9.0e15
EPS = 1e-5
HUGE = 3.0e38
HEADS = 6


def first_jobs():
    stacks = [("k", 0, s) for s in range(4)] + [("q", 0, 0)]
    stacks += [("k", 1, s) for s in range(4)] + [("q", 1, 0)]
    stacks += [("k", 2, s) for s in range(4)] + [("q", 2, 0)]
    jobs = stacks[:7]
    for tile, stack in enumerate(stacks[7:]):
        jobs += [("v", tile, 0), stack]
    return jobs


def batch_steps(units, with_next):
    steps = []
    for t in range(units):
        steps.append(("scores", t))
        if t >= 2:
            steps.append(("turn", t - 2))
        steps.append(("exp", t))
        if t >= 6:
            steps.append(("mix", (t - 6) // 4, (t - 6) % 4))
        if t % 4 == 1 and t >= 5:
            steps.append(("denominators", (t - 5) // 4))
        if t % 4 == 2 and t >= 6:
            steps.append(("spread", (t - 6) // 4))
        if t % 4 == 1 and t >= 9:
            steps.append(("context", (t - 9) // 4))
        if t % 4 == 2 and 6 <= t <= 38:
            n = (t - 6) // 4
            steps.append(("job", ("q", n % 3, 1 + n // 3)))
        if t >= 20 and (t - 20) % 12 < 2:
            steps.append(("project", (t - 20) // 12, (t - 20) % 12))
        if t >= 22 and (t - 22) % 12 == 0:
            steps.append(("deviation", (t - 22) // 12))
        if t >= 23 and (t - 23) % 12 == 0:
            steps.append(("normalise", (t - 23) // 12))
        if 8 <= t < 12:
            steps.append(("residual", t - 8))
        if t == 12 and with_next:
            steps.append(("load x",))
        if t % 12 >= 10 and (t < 40 or with_next):
            steps.append(("mask", t // 12 + 1, t % 12 - 10))
        if with_next and 39 <= t < 47:
            steps.append(("job", ("x", t - 39, 0)))
    pairs = units // 4
    jobs = [("job", j) for j in first_jobs()] if with_next else []
    steps += [("turn", units - 2), ("mix", pairs - 2, 2)] + jobs[:2]
    steps += [("turn", units - 1), ("mix", pairs - 2, 3), ("context", pairs - 2)] + jobs[2:4]
    steps += [("denominators", pairs - 1), ("mix", pairs - 1, 0)] + jobs[4:5]
    steps += [("spread", pairs - 1), ("mix", pairs - 1, 1)] + jobs[5:6]
    steps += [("mix", pairs - 1, 2)] + jobs[6:7]
    steps += [("mix", pairs - 1, 3), ("context", pairs - 1)] + jobs[7:11]
    steps += [("project", 3, 0), ("project", 3, 1)] + jobs[11:13]
    steps += [("deviation", 3)] + jobs[13:14] + [("normalise", 3)] + jobs[14:]
    return steps


def graph_attention(nc, x, adj, wq, bq, wk, bk, wv, bv, wf, bf, out):
    BATCH, S, H = x.shape
    FT = H // P
    TT = S // P
    HS = H // HEADS
    GQ = 2 * P
    UNITS = HEADS * TT
    PAIRS = UNITS // 4
    assert (S, H, HS, FT) == (1024, 384, 64, 3)
    SCALE = -1.0 / 8.0

    first = first_jobs()
    start_jobs = [("x", n, 0) for n in range(TT)] + first
    loop_jobs = [("q", n % 3, 1 + n // 3) for n in range(9)] + start_jobs
    start_stacks = [j for j in start_jobs if j[0] in "kq"]
    loop_stacks = [j for j in loop_jobs if j[0] in "kq"]
    start_splits = [j for j in start_jobs if j[0] != "v"]
    loop_splits = [j for j in loop_jobs if j[0] != "v"]
    COPIES = {"k": 4, "q": 8}

    x_tiles = x.rearrange("b (t p) h -> b p t h", p=P)
    out_tiles = out.rearrange("b (t p) h -> b p t h", p=P)
    adj_rows = adj.rearrange("b s k -> (b s) k")
    spread_dram = nc.dram_tensor("spread_dram", [2, 4, P], F32, kind="Internal").ap()

    with ExitStack() as ctx:
        def sb(name, shape, dt):
            return ctx.enter_context(nc.sbuf_tensor(name, shape, dt))

        def sem(name):
            return ctx.enter_context(nc.semaphore(name))

        k_stack = sb("k_stack", [P, HEADS, S], F32R)
        q_home = sb("q_home", [P, HEADS, GQ], F32R)
        q_swap = sb("q_swap", [P, HEADS, GQ], F32R)
        v_all = sb("v_all", [P, TT, H], F32)
        xt_hi = sb("xt_hi", [P, FT, S], F32R)
        xt_lo = sb("xt_lo", [P, FT, S], F32R)
        weight_hi = sb("weight_hi", [P, 4, FT, H], F32R)
        weight_lo = sb("weight_lo", [P, 4, FT, H], F32R)
        x_in = sb("x_in", [P, TT, H], F32)
        res = sb("res", [P, TT, H], F32)
        adj_in = sb("adj_in", [P, 2, S], U8)
        mask = sb("mask", [P, 2, S], F32)
        prob = sb("prob", [P, 3, S], F32)
        prob_t = sb("prob_t", [P, 2, 2, TT, GQ], F32)
        part_hi = sb("part_hi", [P, 2, GQ], F32R)
        part_lo = sb("part_lo", [P, 2, GQ], F32R)
        context = sb("context", [P, GQ], F32)
        context_hi = sb("context_hi", [P, FT, GQ], F32R)
        context_lo = sb("context_lo", [P, FT, GQ], F32R)
        inv_rows = sb("inv_rows", [P, 2, GQ], F32)
        ident = sb("ident", [P, P], F32)
        bias_raw = sb("bias_raw", [P, 2, FT], F32)
        bias_qk = sb("bias_qk", [P, 2, FT], F32)
        bv_rows = sb("bv_rows", [P, H], F32)
        bf_rows = sb("bf_rows", [P, H], F32)
        row_min = sb("row_min", [P, 4], F32)
        row_sum = sb("row_sum", [P, 2, 4], F32)
        inv_sum = sb("inv_sum", [P, 2, 4], F32)
        stats = sb("stats", [P, 2, 6], F32)
        mean_var = sb("mean_var", [P, 2, 2], F32)
        var_eps = sb("var_eps", [P, 2], F32)
        deviation = sb("deviation", [P, 2], F32)
        inv_dev = sb("inv_dev", [P, 2], F32)

        score_ps = ctx.enter_context(nc.psum_tensor("score_ps", [P, 2, S], F32))
        turn_ps = ctx.enter_context(nc.psum_tensor("turn_ps", [P, 2, 4, P], F32))
        context_ps = ctx.enter_context(nc.psum_tensor("context_ps", [P, 512], F32))
        misc_ps = ctx.enter_context(nc.psum_tensor("misc_ps", [P, 512], F32))
        weight_raw = prob_t[:].rearrange("p a b c d -> p (a b c d)")[:, 0:4 * FT * H].rearrange(
            "p (w t h) -> p w t h", w=4, t=FT)

        weights_in = sem("weights_in")
        biases_in = sem("biases_in")
        bias_scaled = sem("bias_scaled")
        weights_hi_done = sem("weights_hi_done")
        weights_done = sem("weights_done")
        ident_clear = sem("ident_clear")
        ident_done = sem("ident_done")
        x_loaded = sem("x_loaded")
        adj_loaded = [sem(f"adj_loaded{i}") for i in range(2)]
        mask_done = sem("mask_done")
        scores_done = sem("scores_done")
        masked = sem("masked")
        exp_done = sem("exp_done")
        turned = [sem(f"turned{i}") for i in range(2)]
        copied = [sem(f"copied{i}") for i in range(2)]
        mixed = sem("mixed")
        inv_done = sem("inv_done")
        spread_out = [sem(f"spread_out{i}") for i in range(2)]
        spread_in = [sem(f"spread_in{i}") for i in range(2)]
        context_done = sem("context_done")
        context_hi_done = sem("context_hi_done")
        context_lo_done = sem("context_lo_done")
        job_done = sem("job_done")
        hi_done = sem("hi_done")
        job_out = sem("job_out")
        stacked = [sem(f"stacked{i}") for i in range(2)]
        projected = sem("projected")
        res_done = sem("res_done")
        sum_done = sem("sum_done")
        stats_done = sem("stats_done")
        mean_done = sem("mean_done")
        var_done = sem("var_done")
        deviation_done = sem("deviation_done")
        inv_dev_done = sem("inv_dev_done")
        normalised = sem("normalised")
        dve_waited = sem("dve_waited")
        pool_waited = sem("pool_waited")
        stored = [sem(f"stored{g}") for g in range(4)]

        def jobs_through(b, job, per=(start_jobs, loop_jobs)):
            before, loop = per
            if b is None:
                return before.index(job) + 1
            return b * len(loop) + (len(before) + loop.index(job) + 1)

        def copies_through(b, job, slot):
            def total(jobs, offset):
                return sum(16 * COPIES[j[0]] for n, j in enumerate(jobs) if (n + offset) % 2 == slot)
            if b is None:
                return total(start_stacks[:start_stacks.index(job) + 1], 0)
            n = len(start_stacks)
            return b * total(loop_stacks, n) + (
                total(start_stacks, 0) + total(loop_stacks[:loop_stacks.index(job) + 1], n))

        def stack_slot(b, job):
            n = start_stacks.index(job) if b is None else len(start_stacks) + loop_stacks.index(job)
            return n % 2

        def wait_part_slot(eng, b, job):
            jobs = start_stacks if b is None else loop_stacks
            n, slot = jobs.index(job), stack_slot(b, job)
            if n >= 2:
                eng.wait_ge(stacked[slot], copies_through(b, jobs[n - 2], slot))
            elif b is not None:
                eng.wait_ge(stacked[slot], first_copies(b, start_stacks[-1], slot))

        def first_jobs_through(b, job):
            return b * len(loop_jobs) + (start_jobs.index(job) + 1)

        def first_copies(b, job, slot):
            def total(jobs):
                return sum(16 * COPIES[j[0]] for n, j in jobs)
            in_slot = [(n, j) for n, j in enumerate(start_stacks) if n % 2 == slot]
            begun = total((n, j) for n, j in in_slot if n <= start_stacks.index(job))
            each = total(in_slot) + total((n, j) for n, j in enumerate(loop_stacks[:9])
                                          if (n + len(start_stacks)) % 2 == slot)
            return b * each + begun

        def job_bank(job, width=GQ):
            if job in first:
                k = first.index(job)
                return score_ps[:, (k % 4) // 2, (k % 2) * 512:(k % 2) * 512 + width]
            return misc_ps[:, 0:width]

        block = ctx.enter_context(nc.Block())

        @block.sync
        def _(sp):
            for w, src in enumerate((wq, wk, wv, wf)):
                sp.dma_start(weight_raw[:, w], src.rearrange("(t p) n -> p t n", p=P)).then_inc(weights_in, 16)
            sp.dma_start(x_in[:], x_tiles[0]).then_inc(x_loaded, 16)
            for n, src in enumerate((bq, bk)):
                sp.dma_start(bias_raw[:, n, :], src.rearrange("(t p) -> p t", p=P),
                             allow_slow_non_contiguous=True).then_inc(biases_in, 16)
            sp.dma_start(bv_rows[:], bv.partition_broadcast(P)).then_inc(biases_in, 16)
            sp.dma_start(bf_rows[:], bf.partition_broadcast(P)).then_inc(biases_in, 16)
            for qt in range(2):
                sp.dma_start(adj_in[:, qt, :], adj_rows[qt * P:(qt + 1) * P, :]).then_inc(adj_loaded[qt], 16)
            for g in range(4):
                sp.sem_inc(stored[g], 16)

            def stack(b, job):
                sp.wait_ge(job_out, jobs_through(b, job))
                kind, pair, piece = job
                slot = stack_slot(b, job)
                a, c = 2 * pair, 2 * pair + 1
                if kind == "k":
                    cols = slice(piece * GQ, (piece + 1) * GQ)
                    lay = [(k_stack, cols, part_hi, part_lo)]
                else:
                    cols = slice(0, GQ)
                    lay = [(q_home, cols, part_hi, part_lo), (q_swap, cols, part_lo, part_hi)]
                for dst, at, own, other in lay:
                    for to, head, src, rows in ((0, a, own, 0), (64, a, other, 0),
                                                (64, c, own, 64), (0, c, other, 64)):
                        sp.dma_start(dst[to:to + 64, head, at].bitcast(F32),
                                     src[rows:rows + 64, slot, :].bitcast(F32)).then_inc(stacked[slot], 16)

            def body(b, with_next):
                for step in batch_steps(UNITS, with_next):
                    kind = step[0]
                    if kind == "job" and step[1][0] in "kq":
                        stack(b, step[1])
                    elif kind == "denominators":
                        pair = step[1]
                        sp.wait_ge(inv_done, b * PAIRS + (pair + 1))
                        sp.wait_ge(context_done, b * PAIRS + (pair + 1))
                        sp.dma_start(spread_dram[pair % 2].rearrange("c p -> p c"), inv_sum[:, pair % 2, :],
                                     allow_slow_non_contiguous=True).then_inc(spread_out[pair % 2], 16)
                    elif kind == "spread":
                        pair = step[1]
                        sp.wait_ge(spread_out[pair % 2], b * (8 * PAIRS) + 16 * (pair // 2 + 1))
                        for head in range(2):
                            src = spread_dram[pair % 2, 2 * head:2 * head + 2, :].rearrange("c p -> (c p)")
                            sp.dma_start(inv_rows[64 * head:64 * head + 64, pair % 2, :],
                                         src.partition_broadcast(64)).then_inc(spread_in[pair % 2], 16)
                    elif kind == "mask":
                        group, qt = step[1:]
                        if not with_next and group == 3:
                            continue
                        sp.wait_ge(mask_done, b * 8 + (2 * group + qt + 1))
                        sp.dma_start(adj_in[:, qt, :],
                                     adj_rows[bass.ds(b * S + ((group + 1) * GQ + qt * P), P), :]
                                     ).then_inc(adj_loaded[qt], 16)
                    elif kind == "load x":
                        sp.wait_ge(res_done, b * TT + TT)
                        sp.dma_start(x_in[:], x_tiles[b + 1]).then_inc(x_loaded, 16)
                    elif kind == "normalise":
                        group = step[1]
                        sp.wait_ge(normalised, b * TT + 2 * (group + 1))
                        sp.dma_start(out_tiles[b, :, 2 * group:2 * group + 2, :],
                                     res[:, 2 * group:2 * group + 2, :]).then_inc(stored[group], 16)

            sp.wait_ge(mask_done, 2)
            for qt in range(2):
                sp.dma_start(adj_in[:, qt, :],
                             adj_rows[GQ + qt * P:GQ + (qt + 1) * P, :]).then_inc(adj_loaded[qt], 16)
            for job in start_stacks:
                stack(None, job)
            with sp.Fori(0, BATCH - 1) as b:
                body(b, True)
            body(BATCH - 1, False)
            for g in range(4):
                sp.wait_ge(stored[g], 16 * (BATCH + 1))

        @block.tensor
        def _(pe):
            pe.sem_inc(turned[1], 3)
            pe.sem_inc(mixed, 2)
            pe.sem_inc(projected, 1)

            def three_products(dst, pieces):
                for t, (left_hi, left_lo, right_hi, right_lo) in enumerate(pieces):
                    pe.matmul(dst, left_hi, right_hi, start=(t == 0), stop=False)
                    pe.matmul(dst, left_hi, right_lo, start=False, stop=False)
                    last = pe.matmul(dst, left_lo, right_hi, start=False, stop=(t == FT - 1))
                return last

            def wait_misc(b, last_job, sums):
                if last_job is not None:
                    pe.wait_ge(job_out, last_job)
                if b is not None:
                    pe.wait_ge(sum_done, b * TT + (sums + 1))

            def transpose_x(b, tile, last_job, sums):
                if tile == 0:
                    pe.wait_ge(x_loaded, 16 if b is None else b * 16 + 32)
                wait_misc(b, last_job, sums)
                for t in range(FT):
                    last = pe.transpose(misc_ps[:, t * P:(t + 1) * P], x_in[:, tile, t * P:(t + 1) * P], ident[:])
                last.then_inc(job_done, 1)

            def wait_score_bank(b, job):
                k = first.index(job)
                if k == 0:
                    pe.wait_ge(job_out, jobs_through(b, ("x", TT - 1, 0)))
                if k >= 4:
                    pe.wait_ge(job_out, jobs_through(b, first[k - 4]))
                elif b is not None:
                    pe.wait_ge(masked, b * UNITS + (UNITS + 1 + k // 2))
                return score_ps[:, (k % 4) // 2, (k % 2) * 512:(k % 2) * 512 + 512]

            def project_qk(dst, kind, pair, piece):
                w = 1 if kind == "k" else 0
                feat = slice(pair * P, (pair + 1) * P)
                tok = slice(piece * GQ, (piece + 1) * GQ)
                three_products(dst[:, 0:GQ], [
                    (weight_hi[:, w, t, feat], weight_lo[:, w, t, feat], xt_hi[:, t, tok], xt_lo[:, t, tok])
                    for t in range(FT)]).then_inc(job_done, 1)

            def project_v(dst, tile):
                tok = slice(tile * P, (tile + 1) * P)
                three_products(dst[:, 0:H], [
                    (xt_hi[:, t, tok], xt_lo[:, t, tok], weight_hi[:, 2, t, :], weight_lo[:, 2, t, :])
                    for t in range(FT)]).then_inc(job_done, 1)

            def first_job(b, job):
                dst = wait_score_bank(b, job)
                if job[0] == "v":
                    project_v(dst, job[1])
                else:
                    project_qk(dst, *job)

            def body(b, with_next):
                sums = 0
                misc_job = first_jobs_through(b, start_jobs[-1])
                for step in batch_steps(UNITS, with_next):
                    kind = step[0]
                    if kind == "scores":
                        t = step[1]
                        group, pair, head, qt = t // 12, t % 12 // 4, t % 2, t % 4 // 2
                        h = 2 * pair + head
                        pe.wait_ge(masked, b * UNITS + (t + 1))
                        if t < 2:
                            pe.wait_ge(job_out, first_jobs_through(b, first[21 + t]))
                        if t % 4 == 0 and group == 0:
                            for slot in range(2):
                                pe.wait_ge(stacked[slot], first_copies(b, ("q", pair, 0), slot))
                        elif t % 4 == 0:
                            slot = stack_slot(b, ("q", pair, group))
                            pe.wait_ge(stacked[slot], copies_through(b, ("q", pair, group), slot))
                        q = slice(qt * P, (qt + 1) * P)
                        for n, q_stack in enumerate((q_home, q_swap)):
                            for half in range(2):
                                keys = slice(half * 512, half * 512 + 512)
                                last = pe.matmul(score_ps[:, t % 2, keys], q_stack[:, h, q], k_stack[:, h, keys],
                                                 start=(n == 0), stop=(n == 1))
                        last.then_inc(scores_done, 1)
                    elif kind == "turn":
                        u = step[1]
                        pe.wait_ge(exp_done, b * UNITS + (u + 1))
                        for half in range(2):
                            pe.wait_ge(copied[half], b * UNITS + (u + 1))
                            for i in range(4):
                                kt = 4 * half + i
                                last = pe.transpose(turn_ps[:, half, i, :], prob[:, u % 3, kt * P:(kt + 1) * P],
                                                    ident[:])
                            last.then_inc(turned[half], 1)
                    elif kind == "mix":
                        pair, chunk = step[1:]
                        if chunk == 0:
                            if pair == 0:
                                pe.wait_ge(job_out, first_jobs_through(b, ("v", TT - 1, 0)))
                            for half in range(2):
                                pe.wait_ge(copied[half], b * UNITS + (4 * pair + 5))
                            pe.wait_ge(context_done, b * PAIRS + (pair + 2))
                        for kt in (2 * chunk, 2 * chunk + 1):
                            for head in range(2):
                                col = (2 * (pair % 3) + head) * HS
                                last = pe.matmul(context_ps[64 * head:64 * head + 64, 0:GQ],
                                                 v_all[:, kt, col:col + HS], prob_t[:, pair % 2, head, kt, :],
                                                 start=(kt == 0), stop=(kt == TT - 1))
                        if chunk == 3:
                            last.then_inc(mixed, 1)
                    elif kind == "job":
                        job = step[1]
                        if job[0] == "x":
                            transpose_x(b, job[1], misc_job, sums)
                            misc_job = jobs_through(b, job)
                        elif job in first:
                            first_job(b, job)
                        else:
                            wait_misc(b, misc_job, sums)
                            project_qk(misc_ps, *job)
                            misc_job = jobs_through(b, job)
                    elif kind == "project":
                        group, tile = step[1:]
                        wait_misc(b, misc_job, sums)
                        if tile == 0:
                            pe.wait_ge(context_lo_done, b * PAIRS + (3 * group + 4))
                        tok = slice(tile * P, (tile + 1) * P)
                        three_products(misc_ps[:, 0:H], [
                            (context_hi[:, t, tok], context_lo[:, t, tok], weight_hi[:, 3, t, :],
                             weight_lo[:, 3, t, :]) for t in range(FT)]).then_inc(projected, 1)
                        sums += 1

            pe.wait_ge(ident_done, 1)
            for tile in range(TT):
                transpose_x(None, tile, tile or None, 0)
            pe.wait_ge(weights_done, 4)
            for job in first:
                first_job(None, job)
            with pe.Fori(0, BATCH - 1) as b:
                body(b, True)
            body(BATCH - 1, False)

        @block.scalar
        def _(act):
            act.sem_inc(copied[0], 1)

            def high_part(b, job):
                kind, n, piece = job
                act.wait_ge(job_done, jobs_through(b, job))
                if kind == "x":
                    src = misc_ps[:, 0:H].rearrange("p (t q) -> p t q", t=FT)
                    nc.scalar.activation(xt_hi[:, :, n * P:(n + 1) * P], src, ACT.Copy).then_inc(hi_done, 1)
                    return
                wait_part_slot(act, b, job)
                w = 1 if kind == "k" else 0
                nc.scalar.activation(part_hi[:, stack_slot(b, job), :], job_bank(job), ACT.Identity,
                                     bias=bias_qk[:, w, n:n + 1]).then_inc(hi_done, 1)

            def body(b, with_next):
                for step in batch_steps(UNITS, with_next):
                    kind = step[0]
                    if kind == "turn":
                        u = step[1]
                        pair, head, qt = u // 4, u % 2, u % 4 // 2
                        if u % 4 == 0:
                            act.wait_ge(mixed, b * PAIRS + (pair + 1))
                        act.wait_ge(turned[0], b * UNITS + (u + 1))
                        nc.scalar.activation(prob_t[:, pair % 2, head, 0:4, qt * P:(qt + 1) * P],
                                             turn_ps[:, 0], ACT.Copy).then_inc(copied[0], 1)
                    elif kind == "exp":
                        t = step[1]
                        col = 2 * (t % 2) + t % 4 // 2
                        act.wait_ge(masked, b * UNITS + (t + 3))
                        nc.scalar.activation(prob[:, t % 3, :], prob[:, t % 3, :], ACT.Exp, scale=-1.0,
                                             bias=row_min[:, t % 4:t % 4 + 1],
                                             accum_out=row_sum[:, t // 4 % 2, col:col + 1]).then_inc(exp_done, 1)
                    elif kind == "job" and step[1][0] != "v":
                        high_part(b, step[1])
                    elif kind == "context":
                        pair = step[1]
                        act.wait_ge(context_done, b * PAIRS + (pair + 3))
                        if pair % 3 == 0:
                            act.wait_ge(projected, b * TT + (2 * (pair // 3) + 1))
                        nc.scalar.activation(context_hi[:, pair % 3, :], context[:],
                                             ACT.Copy).then_inc(context_hi_done, 1)
                    elif kind == "deviation":
                        act.wait_ge(var_done, b * 4 + (step[1] + 1))
                        nc.scalar.activation(deviation[:], var_eps[:], ACT.Sqrt).then_inc(deviation_done, 1)

            act.wait_ge(weights_in, 64)
            for w in range(4):
                nc.scalar.activation(weight_hi[:, w], weight_raw[:, w], ACT.Copy,
                                     scale=SCALE if w == 0 else 1.0).then_inc(weights_hi_done, 1)
            act.wait_ge(bias_scaled, 2)
            for job in start_splits:
                high_part(None, job)
            with act.Fori(0, BATCH - 1) as b:
                body(b, True)
            body(BATCH - 1, False)

        @block.vector
        def _(dve):
            dve.sem_inc(masked, 2)
            dve.sem_inc(copied[1], 1)
            dve.sem_inc(context_done, 2)
            dve.sem_inc(sum_done, 1)

            def job_result(b, job):
                kind, n, piece = job
                if kind == "v":
                    dve.wait_ge(job_done, jobs_through(b, job))
                    nc.vector.tensor_tensor(v_all[:, n, :], job_bank(job, H), bv_rows[:], ALU.add).then_inc(job_out, 1)
                    return
                dve.wait_ge(hi_done, jobs_through(b, job, (start_splits, loop_splits)))
                if kind == "x":
                    tok = slice(n * P, (n + 1) * P)
                    src = misc_ps[:, 0:H].rearrange("p (t q) -> p t q", t=FT)
                    nc.vector.tensor_tensor(xt_lo[:, :, tok], src, xt_hi[:, :, tok], ALU.subtract).then_inc(job_out, 1)
                    return
                w, slot = (1 if kind == "k" else 0), stack_slot(b, job)
                nc.vector.scalar_tensor_tensor(out=part_lo[:, slot, :], in0=job_bank(job),
                                               scalar=bias_qk[:, w, n:n + 1], in1=part_hi[:, slot, :],
                                               op0=ALU.add, op1=ALU.subtract).then_inc(job_out, 1)

            def body(b, with_next):
                for step in batch_steps(UNITS, with_next):
                    kind = step[0]
                    if kind == "scores":
                        t = step[1]
                        qt = t % 4 // 2
                        dve.wait_ge(scores_done, b * UNITS + (t + 1))
                        dve.wait_ge(turned[1], b * UNITS + (t + 1))
                        if t % 12 in (0, 2):
                            dve.wait_ge(mask_done, b * TT + (2 * (t // 12) + qt + 1))
                        dve.sem_inc(dve_waited, 1)
                        nc.vector.tensor_tensor_reduce(prob[:, t % 3, :], score_ps[:, t % 2, :], mask[:, qt, :],
                                                       1.0, HUGE, ALU.add, ALU.min,
                                                       row_min[:, t % 4:t % 4 + 1]).then_inc(masked, 1)
                    elif kind == "turn":
                        u = step[1]
                        pair, head, qt = u // 4, u % 2, u % 4 // 2
                        if u % 4 == 0:
                            dve.wait_ge(mixed, b * PAIRS + (pair + 1))
                        dve.wait_ge(turned[1], b * UNITS + (u + 4))
                        nc.vector.tensor_copy(prob_t[:, pair % 2, head, 4:8, qt * P:(qt + 1) * P],
                                              turn_ps[:, 1]).then_inc(copied[1], 1)
                    elif kind == "denominators":
                        pair = step[1]
                        dve.wait_ge(exp_done, b * UNITS + 4 * (pair + 1))
                        nc.vector.reciprocal(inv_sum[:, pair % 2, :], row_sum[:, pair % 2, :]).then_inc(inv_done, 1)
                    elif kind == "context":
                        pair = step[1]
                        dve.wait_ge(mixed, b * PAIRS + (pair + 3))
                        dve.wait_ge(spread_in[pair % 2], b * (16 * PAIRS) + 32 * (pair // 2 + 1))
                        dve.wait_ge(context_lo_done, b * PAIRS + (pair + 1))
                        nc.vector.tensor_tensor(context[:], context_ps[:, 0:GQ], inv_rows[:, pair % 2, :],
                                                ALU.mult).then_inc(context_done, 1)
                    elif kind == "job":
                        job_result(b, step[1])
                    elif kind == "project":
                        group, tile = step[1:]
                        n = 2 * group + tile
                        dve.wait_ge(projected, b * TT + (n + 2))
                        dve.wait_ge(res_done, b * TT + (n + 1))
                        nc.vector.tensor_tensor(res[:, n, :], misc_ps[:, 0:H], res[:, n, :],
                                                ALU.add).then_inc(sum_done, 1)
                        dve.wait_ge(sum_done, b * TT + (n + 2))
                        nc.vector.bn_stats(stats[:, tile, :], res[:, n, :]).then_inc(stats_done, 1)
                        dve.wait_ge(stats_done, b * TT + (n + 1))
                        dve.sem_inc(dve_waited, 1)
                        nc.vector.bn_aggr(mean_var[:, tile, :], stats[:, tile, :]).then_inc(mean_done, 1)
                        if tile == 1:
                            dve.wait_ge(mean_done, b * TT + (n + 1))
                            nc.vector.tensor_scalar(var_eps[:], mean_var[:, :, 1], EPS, None,
                                                    ALU.add).then_inc(var_done, 1)
                    elif kind == "normalise":
                        group = step[1]
                        dve.wait_ge(deviation_done, b * 4 + (group + 1))
                        nc.vector.reciprocal(inv_dev[:], deviation[:]).then_inc(inv_dev_done, 1)
                        dve.wait_ge(inv_dev_done, b * 4 + (group + 1))
                        for tile in range(2):
                            n = 2 * group + tile
                            nc.vector.tensor_scalar(res[:, n, :], res[:, n, :], mean_var[:, tile, 0:1],
                                                    inv_dev[:, tile:tile + 1], ALU.subtract,
                                                    ALU.mult).then_inc(normalised, 1)

            dve.wait_ge(biases_in, 64)
            nc.vector.tensor_scalar(bias_qk[:, 0, :], bias_raw[:, 0, :], SCALE, None, ALU.mult).then_inc(bias_scaled, 1)
            nc.vector.tensor_copy(bias_qk[:, 1, :], bias_raw[:, 1, :]).then_inc(bias_scaled, 1)
            for w in range(4):
                dve.wait_ge(weights_hi_done, w + 1)
                nc.vector.scalar_tensor_tensor(out=weight_lo[:, w], in0=weight_raw[:, w],
                                               scalar=SCALE if w == 0 else 1.0, in1=weight_hi[:, w],
                                               op0=ALU.mult, op1=ALU.subtract).then_inc(weights_done, 1)
            dve.wait_ge(bias_scaled, 2)
            for job in start_jobs:
                job_result(None, job)
            with dve.Fori(0, BATCH - 1) as b:
                body(b, True)
            body(BATCH - 1, False)

        @block.gpsimd
        def _(pool):
            pool.sem_inc(context_lo_done, 1)

            def make_mask(qt):
                nc.gpsimd.tensor_scalar(mask[:, qt, :], adj_in[:, qt, :], -NEG, NEG, ALU.mult,
                                        ALU.add).then_inc(mask_done, 1)

            def body(b, with_next):
                for step in batch_steps(UNITS, with_next):
                    kind = step[0]
                    if kind == "mask":
                        group, qt = step[1:]
                        pool.wait_ge(adj_loaded[qt], b * 64 + 16 * (group + 1))
                        pool.wait_ge(masked, b * UNITS + (12 * (group - 1) + 12 + 2 * qt))
                        pool.sem_inc(pool_waited, 1)
                        make_mask(qt)
                    elif kind == "residual":
                        g = step[1]
                        pool.wait_ge(x_loaded, b * 16 + 16)
                        pool.wait_ge(stored[g], b * 16 + 16)
                        for n in (2 * g, 2 * g + 1):
                            nc.gpsimd.tensor_tensor(res[:, n, :], x_in[:, n, :], bf_rows[:],
                                                    ALU.add).then_inc(res_done, 1)
                    elif kind == "context":
                        pair = step[1]
                        pool.wait_ge(context_hi_done, b * PAIRS + (pair + 1))
                        nc.gpsimd.tensor_tensor(context_lo[:, pair % 3, :], context[:], context_hi[:, pair % 3, :],
                                                ALU.subtract).then_inc(context_lo_done, 1)

            nc.gpsimd.memset(ident[:], 0.0).then_inc(ident_clear, 1)
            pool.wait_ge(ident_clear, 1)
            nc.gpsimd.affine_select(out=ident[:], in_=ident[:], compare_op=ALU.not_equal, fill=1.0, base=0,
                                    pattern=[[-1, P]], channel_multiplier=1).then_inc(ident_done, 1)
            for qt in range(2):
                pool.wait_ge(adj_loaded[qt], 16)
                make_mask(qt)
            pool.wait_ge(biases_in, 64)
            with pool.Fori(0, BATCH - 1) as b:
                body(b, True)
            body(BATCH - 1, False)


_INS = ["x", "adj", "L0_gnn_Wq", "L0_gnn_bq", "L0_gnn_Wk", "L0_gnn_bk", "L0_gnn_Wv", "L0_gnn_bv", "L0_gnn_Wf",
        "L0_gnn_bf"]


def kernel(**inputs):
    import numpy as _np
    import concourse.bacc as _bacc
    from concourse.bass_utils import run_bass_kernel_spmd as _run

    nc = _bacc.Bacc("TRN2", target_bir_lowering=False, num_devices=1)
    arrays, args = {}, []
    for name in _INS:
        a = _np.ascontiguousarray(inputs[name])
        arrays[f"in_{name}_dram"] = a
        args.append(nc.dram_tensor(f"in_{name}_dram", a.shape, mybir.dt.from_np(a.dtype), kind="ExternalInput").ap())
    out = nc.dram_tensor("out_0_dram", inputs["x"].shape, F32, kind="ExternalOutput").ap()
    graph_attention(nc, *args, out)
    return _run(nc, [arrays], core_ids=[0]).results[0]["out_0_dram"]
```

```python
from contextlib import ExitStack

import concourse.bass as bass
from concourse import mybir

F32 = mybir.dt.float32
F32R = mybir.dt.float32r
U8 = mybir.dt.uint8
ALU = mybir.AluOpType
ACT = mybir.ActivationFunctionType

P = 128
NEG = 9.0e15
EPS = 1e-5
HUGE = 3.0e38
HEADS = 6


def first_jobs():
    return [job for pair in range(3) for job in (("k", pair, 0), ("k", pair, 1), ("q", pair, 0))]


def batch_steps(units, with_next):
    steps = []
    for t in range(units):
        steps.append(("scores", t))
        if t < 8:
            steps.append(("job", ("v", t, 0)))
        elif t % 4 == 0 and t <= 40:
            steps.append(("job", ("q", (t - 8) // 4 % 3, 1 + (t - 8) // 12)))
        elif t >= 19 and (t - 19) % 12 in (0, 2):
            steps.append(("project", (t - 19) // 12, (t - 19) % 12 // 2))
        elif t >= 41 and with_next:
            steps.append(("job", ("x", t - 41, 0)))
        if t >= 2:
            steps.append(("turn", t - 2))
        steps.append(("exp", t))
        if t >= 7 and t % 2 == 1:
            steps.append(("mix", (t - 7) // 4, (t - 7) % 4 // 2))
        if t % 4 == 1 and t >= 5:
            steps.append(("denominators", (t - 5) // 4))
        if t % 4 == 2 and t >= 6:
            steps.append(("spread", (t - 6) // 4))
        if t % 4 == 1 and t >= 9:
            steps.append(("context", (t - 9) // 4))
        if t in (43, 45) and with_next:
            steps.append(("job", ("x", t - 41, 0)))
        if t >= 22 and (t - 22) % 12 == 0:
            steps.append(("deviation", (t - 22) // 12))
        if t >= 23 and (t - 23) % 12 == 0:
            steps.append(("normalise", (t - 23) // 12))
        if 8 <= t < 12:
            steps.append(("residual", t - 8))
        if t == 12 and with_next:
            steps.append(("load x",))
        if t % 12 >= 10 and (t < 40 or with_next):
            steps.append(("mask", t // 12 + 1, t % 12 - 10))
    jobs = [("job", j) for j in first_jobs()] if with_next else []
    last = units // 4 - 1
    steps += [("job", ("x", 7, 0))] if with_next else []
    steps += [("turn", units - 2)] + jobs[:1] + [("turn", units - 1), ("mix", last - 1, 1)]
    steps += [("denominators", last), ("context", last - 1)] + jobs[1:2]
    steps += [("spread", last), ("mix", last, 0)] + jobs[2:4]
    steps += [("mix", last, 1), ("context", last)] + jobs[4:6]
    steps += [("project", 3, 0), ("project", 3, 1)] + jobs[6:]
    steps += [("deviation", 3), ("normalise", 3)]
    return steps


def graph_attention(nc, x, adj, wq, bq, wk, bk, wv, bv, wf, bf, out):
    BATCH, S, H = x.shape
    FT = H // P
    TT = S // P
    HS = H // HEADS
    GQ = 2 * P
    UNITS = HEADS * TT
    PAIRS = UNITS // 4
    assert (S, H, HS, FT) == (1024, 384, 64, 3)
    SCALE = -1.0 / 8.0

    first = first_jobs()
    start_jobs = [("x", n, 0) for n in range(TT)] + first
    loop_jobs = [("v", n, 0) for n in range(TT)] + [("q", n % 3, 1 + n // 3) for n in range(9)] + start_jobs
    loop_splits = [j for j in loop_jobs if j[0] != "v"]

    x_tiles = x.rearrange("b (t p) h -> b p t h", p=P)
    out_tiles = out.rearrange("b (t p) h -> b p t h", p=P)
    adj_rows = adj.rearrange("b s k -> (b s) k")
    spread_dram = nc.dram_tensor("spread_dram", [2, 4, P], F32, kind="Internal").ap()

    with ExitStack() as ctx:
        def sb(name, shape, dt):
            return ctx.enter_context(nc.sbuf_tensor(name, shape, dt))

        def sem(name):
            return ctx.enter_context(nc.semaphore(name))

        k_stack = sb("k_stack", [P, HEADS, S], F32R)
        q_home = sb("q_home", [P, HEADS, GQ], F32R)
        q_swap = sb("q_swap", [P, HEADS, GQ], F32R)
        v_all = sb("v_all", [P, TT, H], F32)
        xt_hi = sb("xt_hi", [P, FT, S], F32R)
        xt_lo = sb("xt_lo", [P, FT, S], F32R)
        weight_hi = sb("weight_hi", [P, 4, FT, H], F32R)
        weight_lo = sb("weight_lo", [P, 4, FT, H], F32R)
        x_in = sb("x_in", [P, TT, H], F32)
        res = sb("res", [P, TT, H], F32)
        adj_in = sb("adj_in", [P, 2, S], U8)
        mask = sb("mask", [P, 2, S], F32)
        prob = sb("prob", [P, 3, S], F32)
        prob_t = sb("prob_t", [P, 2, 2, TT, GQ], F32)
        context = sb("context", [P, GQ], F32)
        context_hi = sb("context_hi", [P, FT, GQ], F32R)
        context_lo = sb("context_lo", [P, FT, GQ], F32R)
        inv_rows = sb("inv_rows", [P, 2, GQ], F32)
        ident = sb("ident", [P, P], F32)
        bias_raw = sb("bias_raw", [P, 2, FT], F32)
        bias_qk = sb("bias_qk", [P, 2, FT], F32)
        bv_rows = sb("bv_rows", [P, H], F32)
        bf_rows = sb("bf_rows", [P, H], F32)
        row_min = sb("row_min", [P, 4], F32)
        row_sum = sb("row_sum", [P, 2, 4], F32)
        inv_sum = sb("inv_sum", [P, 2, 4], F32)
        stats = sb("stats", [P, 2, 6], F32)
        mean_var = sb("mean_var", [P, 2, 2], F32)
        var_eps = sb("var_eps", [P, 2], F32)
        deviation = sb("deviation", [P, 2], F32)
        inv_dev = sb("inv_dev", [P, 2], F32)

        score_ps = ctx.enter_context(nc.psum_tensor("score_ps", [P, 2, S], F32))
        turn_ps = ctx.enter_context(nc.psum_tensor("turn_ps", [P, 2, 4, P], F32))
        context_ps = ctx.enter_context(nc.psum_tensor("context_ps", [P, 512], F32))
        misc_ps = ctx.enter_context(nc.psum_tensor("misc_ps", [P, 512], F32))
        weight_raw = prob_t[:].rearrange("p a b c d -> p (a b c d)")[:, 0:4 * FT * H].rearrange(
            "p (w t h) -> p w t h", w=4, t=FT)

        weights_in = [sem(f"weights_in{w}") for w in range(4)]
        biases_in = sem("biases_in")
        bias_scaled = sem("bias_scaled")
        weights_hi_done = sem("weights_hi_done")
        weights_done = sem("weights_done")
        ident_clear = sem("ident_clear")
        ident_done = sem("ident_done")
        x_loaded = [sem(f"x_loaded{g}") for g in range(4)]
        adj_loaded = [sem(f"adj_loaded{i}") for i in range(2)]
        mask_done = sem("mask_done")
        scores_done = sem("scores_done")
        masked = sem("masked")
        exp_done = sem("exp_done")
        turned = [sem(f"turned{i}") for i in range(2)]
        copied = [sem(f"copied{i}") for i in range(2)]
        mixed = sem("mixed")
        inv_done = sem("inv_done")
        spread_out = [sem(f"spread_out{i}") for i in range(2)]
        spread_in = [sem(f"spread_in{i}") for i in range(2)]
        context_done = sem("context_done")
        context_hi_done = sem("context_hi_done")
        context_lo_done = sem("context_lo_done")
        job_done = sem("job_done")
        hi_done = sem("hi_done")
        job_out = sem("job_out")
        q_swapped = [sem(f"q_swapped{pair}") for pair in range(3)]
        projected = sem("projected")
        res_done = sem("res_done")
        sum_done = sem("sum_done")
        stats_done = sem("stats_done")
        mean_done = sem("mean_done")
        var_done = sem("var_done")
        deviation_done = sem("deviation_done")
        inv_dev_done = sem("inv_dev_done")
        normalised = sem("normalised")
        dve_waited = sem("dve_waited")
        pool_waited = sem("pool_waited")
        stored = [sem(f"stored{g}") for g in range(4)]

        def jobs_through(b, job, before=start_jobs, loop=loop_jobs):
            if b is None:
                return before.index(job) + 1
            return b * len(loop) + (len(before) + loop.index(job) + 1)

        def splits_through(b, job):
            return jobs_through(b, job, start_jobs, loop_splits)

        def first_jobs_through(b, job):
            return b * len(loop_jobs) + (start_jobs.index(job) + 1)

        def score_bank(job):
            return (first.index(job) + 3) % 4

        def job_bank(job):
            if job in first:
                bank = score_bank(job)
                return score_ps[:, bank // 2, (bank % 2) * 512:(bank % 2) * 512 + 512]
            return misc_ps[:]

        def job_parts(job):
            kind, pair, piece = job
            if kind == "k":
                width, cols, stack = 512, slice(piece * 512, piece * 512 + 512), k_stack
            else:
                width, cols, stack = GQ, slice(0, GQ), q_home
            upper, lower = slice(0, 64), slice(64, P)
            return width, stack, cols, ((2 * pair, upper, lower), (2 * pair + 1, lower, upper))

        block = ctx.enter_context(nc.Block())

        @block.sync
        def _(sp):
            def load_x(b):
                for g in range(4):
                    sp.dma_start(x_in[:, 2 * g:2 * g + 2, :], x_tiles[b, :, 2 * g:2 * g + 2, :]
                                 ).then_inc(x_loaded[g], 16)

            load_x(0)
            for w, src in ((1, wk), (0, wq), (2, wv), (3, wf)):
                sp.dma_start(weight_raw[:, w], src.rearrange("(t p) n -> p t n", p=P)).then_inc(weights_in[w], 16)
            for n, src in enumerate((bq, bk)):
                sp.dma_start(bias_raw[:, n, :], src.rearrange("(t p) -> p t", p=P),
                             allow_slow_non_contiguous=True).then_inc(biases_in, 16)
            sp.dma_start(bv_rows[:], bv.partition_broadcast(P)).then_inc(biases_in, 16)
            sp.dma_start(bf_rows[:], bf.partition_broadcast(P)).then_inc(biases_in, 16)
            for qt in range(2):
                sp.dma_start(adj_in[:, qt, :], adj_rows[qt * P:(qt + 1) * P, :]).then_inc(adj_loaded[qt], 16)
            for g in range(4):
                sp.sem_inc(stored[g], 16)

            def swap_q(b, job):
                pair = job[1]
                sp.wait_ge(job_out, jobs_through(b, job))
                for to, at in ((0, 64), (64, 0)):
                    sp.dma_start(q_swap[to:to + 64, 2 * pair:2 * pair + 2, :].bitcast(F32),
                                 q_home[at:at + 64, 2 * pair:2 * pair + 2, :].bitcast(F32)
                                 ).then_inc(q_swapped[pair], 16)

            def body(b, with_next):
                for step in batch_steps(UNITS, with_next):
                    kind = step[0]
                    if kind == "job" and step[1][0] == "q":
                        swap_q(b, step[1])
                    elif kind == "denominators":
                        pair = step[1]
                        sp.wait_ge(inv_done, b * PAIRS + (pair + 1))
                        sp.wait_ge(context_done, b * PAIRS + (pair + 1))
                        sp.dma_start(spread_dram[pair % 2].rearrange("c p -> p c"), inv_sum[:, pair % 2, :],
                                     allow_slow_non_contiguous=True).then_inc(spread_out[pair % 2], 16)
                    elif kind == "spread":
                        pair = step[1]
                        sp.wait_ge(spread_out[pair % 2], b * (8 * PAIRS) + 16 * (pair // 2 + 1))
                        for head in range(2):
                            src = spread_dram[pair % 2, 2 * head:2 * head + 2, :].rearrange("c p -> (c p)")
                            sp.dma_start(inv_rows[64 * head:64 * head + 64, pair % 2, :],
                                         src.partition_broadcast(64)).then_inc(spread_in[pair % 2], 16)
                    elif kind == "mask":
                        group, qt = step[1:]
                        if not with_next and group == 3:
                            continue
                        sp.wait_ge(mask_done, b * 8 + (2 * group + qt + 1))
                        sp.dma_start(adj_in[:, qt, :],
                                     adj_rows[bass.ds(b * S + ((group + 1) * GQ + qt * P), P), :]
                                     ).then_inc(adj_loaded[qt], 16)
                    elif kind == "load x":
                        sp.wait_ge(res_done, b * TT + TT)
                        load_x(b + 1)
                    elif kind == "normalise":
                        group = step[1]
                        sp.wait_ge(normalised, b * TT + 2 * (group + 1))
                        sp.dma_start(out_tiles[b, :, 2 * group:2 * group + 2, :],
                                     res[:, 2 * group:2 * group + 2, :]).then_inc(stored[group], 16)

            sp.wait_ge(mask_done, 2)
            for qt in range(2):
                sp.dma_start(adj_in[:, qt, :],
                             adj_rows[GQ + qt * P:GQ + (qt + 1) * P, :]).then_inc(adj_loaded[qt], 16)
            for pair in range(3):
                swap_q(None, ("q", pair, 0))
            with sp.Fori(0, BATCH - 1) as b:
                body(b, True)
            body(BATCH - 1, False)
            for g in range(4):
                sp.wait_ge(stored[g], 16 * (BATCH + 1))

        @block.tensor
        def _(pe):
            pe.sem_inc(turned[1], 3)
            pe.sem_inc(mixed, 2)
            pe.sem_inc(projected, 1)

            def three_products(dst, pieces):
                for t, (left_hi, left_lo, right_hi, right_lo) in enumerate(pieces):
                    pe.matmul(dst, left_hi, right_hi, start=(t == 0), stop=False)
                    pe.matmul(dst, left_hi, right_lo, start=False, stop=False)
                    last = pe.matmul(dst, left_lo, right_hi, start=False, stop=(t == FT - 1))
                return last

            def wait_misc(b, last_job, sums):
                if last_job is not None:
                    pe.wait_ge(job_out, last_job)
                if b is not None:
                    pe.wait_ge(sum_done, b * TT + (sums + 1))

            def transpose_x(b, tile, last_job, sums):
                if tile % 2 == 0:
                    pe.wait_ge(x_loaded[tile // 2], 16 if b is None else b * 16 + 32)
                wait_misc(b, last_job, sums)
                for t in range(FT):
                    last = pe.transpose(misc_ps[:, t * P:(t + 1) * P], x_in[:, tile, t * P:(t + 1) * P], ident[:])
                last.then_inc(job_done, 1)

            def wait_score_bank(b, job):
                k = first.index(job)
                if k == 0:
                    pe.wait_ge(job_out, jobs_through(b, ("x", TT - 1, 0)))
                if k >= 4:
                    pe.wait_ge(job_out, jobs_through(b, first[k - 4]))
                elif b is not None:
                    pe.wait_ge(masked, b * UNITS + (UNITS + 1 + score_bank(job) // 2))

            def project_qk(kind, pair, piece):
                w, width = (1, 512) if kind == "k" else (0, GQ)
                feat = slice(pair * P, (pair + 1) * P)
                tok = slice(piece * width, (piece + 1) * width)
                three_products(job_bank((kind, pair, piece))[:, 0:width], [
                    (weight_hi[:, w, t, feat], weight_lo[:, w, t, feat], xt_hi[:, t, tok], xt_lo[:, t, tok])
                    for t in range(FT)]).then_inc(job_done, 1)

            def project_v(tile):
                tok = slice(tile * P, (tile + 1) * P)
                three_products(misc_ps[:, 0:H], [
                    (xt_hi[:, t, tok], xt_lo[:, t, tok], weight_hi[:, 2, t, :], weight_lo[:, 2, t, :])
                    for t in range(FT)]).then_inc(job_done, 1)

            def body(b, with_next):
                sums = 0
                misc_job = first_jobs_through(b, start_jobs[-1])
                for step in batch_steps(UNITS, with_next):
                    kind = step[0]
                    if kind == "scores":
                        t = step[1]
                        group, pair, head, qt = t // 12, t % 12 // 4, t % 2, t % 4 // 2
                        h = 2 * pair + head
                        pe.wait_ge(masked, b * UNITS + (t + 1))
                        if t < 2:
                            pe.wait_ge(job_out, first_jobs_through(b, first[6 + 2 * t]))
                        if t % 4 == 0:
                            pe.wait_ge(q_swapped[pair], b * 128 + 32 * (group + 1))
                        q = slice(qt * P, (qt + 1) * P)
                        for n, q_stack in enumerate((q_home, q_swap)):
                            for half in range(2):
                                keys = slice(half * 512, half * 512 + 512)
                                last = pe.matmul(score_ps[:, t % 2, keys], q_stack[:, h, q], k_stack[:, h, keys],
                                                 start=(n == 0), stop=(n == 1))
                        last.then_inc(scores_done, 1)
                    elif kind == "turn":
                        u = step[1]
                        pe.wait_ge(exp_done, b * UNITS + (u + 1))
                        for half in range(2):
                            pe.wait_ge(copied[half], b * UNITS + (u + 1))
                            for i in range(4):
                                kt = 4 * half + i
                                last = pe.transpose(turn_ps[:, half, i, :], prob[:, u % 3, kt * P:(kt + 1) * P],
                                                    ident[:])
                            last.then_inc(turned[half], 1)
                    elif kind == "mix":
                        pair, chunk = step[1:]
                        if chunk == 0:
                            for half in range(2):
                                pe.wait_ge(copied[half], b * UNITS + (4 * pair + 5))
                            pe.wait_ge(context_done, b * PAIRS + (pair + 2))
                        if pair == 0:
                            pe.wait_ge(job_out, jobs_through(b, ("v", 4 * chunk + 3, 0)))
                        for kt in range(4 * chunk, 4 * chunk + 4):
                            for head in range(2):
                                col = (2 * (pair % 3) + head) * HS
                                last = pe.matmul(context_ps[64 * head:64 * head + 64, 0:GQ],
                                                 v_all[:, kt, col:col + HS], prob_t[:, pair % 2, head, kt, :],
                                                 start=(kt == 0), stop=(kt == TT - 1))
                        if chunk == 1:
                            last.then_inc(mixed, 1)
                    elif kind == "job":
                        job = step[1]
                        if job[0] == "x":
                            transpose_x(b, job[1], misc_job, sums)
                            misc_job = jobs_through(b, job)
                        elif job in first:
                            wait_score_bank(b, job)
                            project_qk(*job)
                        else:
                            wait_misc(b, misc_job, sums)
                            if job[0] == "v":
                                project_v(job[1])
                            else:
                                project_qk(*job)
                            misc_job = jobs_through(b, job)
                    elif kind == "project":
                        group, tile = step[1:]
                        wait_misc(b, misc_job, sums)
                        if tile == 0:
                            pe.wait_ge(context_lo_done, b * PAIRS + (3 * group + 4))
                        tok = slice(tile * P, (tile + 1) * P)
                        three_products(misc_ps[:, 0:H], [
                            (context_hi[:, t, tok], context_lo[:, t, tok], weight_hi[:, 3, t, :],
                             weight_lo[:, 3, t, :]) for t in range(FT)]).then_inc(projected, 1)
                        sums += 1

            pe.wait_ge(ident_done, 1)
            for tile in range(TT):
                transpose_x(None, tile, tile or None, 0)
            for job in first:
                pe.wait_ge(weights_done, 1 if job[0] == "k" else 2)
                wait_score_bank(None, job)
                project_qk(*job)
            pe.wait_ge(weights_done, 4)
            with pe.Fori(0, BATCH - 1) as b:
                body(b, True)
            body(BATCH - 1, False)

        @block.scalar
        def _(act):
            act.sem_inc(copied[0], 1)

            def high_part(b, job):
                kind, n, piece = job
                act.wait_ge(job_done, jobs_through(b, job))
                if kind == "x":
                    src = misc_ps[:, 0:H].rearrange("p (t q) -> p t q", t=FT)
                    nc.scalar.activation(xt_hi[:, :, n * P:(n + 1) * P], src, ACT.Copy).then_inc(hi_done, 1)
                    return
                width, stack, cols, heads = job_parts(job)
                for head, rows, _ in heads:
                    last = nc.scalar.activation(stack[rows, head, cols], job_bank(job)[rows, 0:width], ACT.Identity,
                                                bias=bias_qk[rows, 1 if kind == "k" else 0, n:n + 1])
                last.then_inc(hi_done, 1)

            def body(b, with_next):
                for step in batch_steps(UNITS, with_next):
                    kind = step[0]
                    if kind == "turn":
                        u = step[1]
                        pair, head, qt = u // 4, u % 2, u % 4 // 2
                        if u % 4 == 0:
                            act.wait_ge(mixed, b * PAIRS + (pair + 1))
                        act.wait_ge(turned[0], b * UNITS + (u + 1))
                        nc.scalar.activation(prob_t[:, pair % 2, head, 0:4, qt * P:(qt + 1) * P],
                                             turn_ps[:, 0], ACT.Copy).then_inc(copied[0], 1)
                    elif kind == "exp":
                        t = step[1]
                        col = 2 * (t % 2) + t % 4 // 2
                        act.wait_ge(masked, b * UNITS + (t + 3))
                        nc.scalar.activation(prob[:, t % 3, :], prob[:, t % 3, :], ACT.Exp, scale=-1.0,
                                             bias=row_min[:, t % 4:t % 4 + 1],
                                             accum_out=row_sum[:, t // 4 % 2, col:col + 1]).then_inc(exp_done, 1)
                    elif kind == "job" and step[1][0] != "v":
                        high_part(b, step[1])
                    elif kind == "context":
                        pair = step[1]
                        act.wait_ge(context_done, b * PAIRS + (pair + 3))
                        if pair % 3 == 0:
                            act.wait_ge(projected, b * TT + (2 * (pair // 3) + 1))
                        nc.scalar.activation(context_hi[:, pair % 3, :], context[:],
                                             ACT.Copy).then_inc(context_hi_done, 1)
                    elif kind == "deviation":
                        act.wait_ge(var_done, b * 4 + (step[1] + 1))
                        nc.scalar.activation(deviation[:], var_eps[:], ACT.Sqrt).then_inc(deviation_done, 1)

            for w in (1, 0, 2, 3):
                act.wait_ge(weights_in[w], 16)
                nc.scalar.activation(weight_hi[:, w], weight_raw[:, w], ACT.Copy,
                                     scale=SCALE if w == 0 else 1.0).then_inc(weights_hi_done, 1)
            act.wait_ge(bias_scaled, 2)
            for job in start_jobs:
                high_part(None, job)
            with act.Fori(0, BATCH - 1) as b:
                body(b, True)
            body(BATCH - 1, False)

        @block.vector
        def _(dve):
            dve.sem_inc(masked, 2)
            dve.sem_inc(copied[1], 1)
            dve.sem_inc(context_done, 2)
            dve.sem_inc(sum_done, 1)

            def job_result(b, job):
                kind, n, piece = job
                if kind == "v":
                    dve.wait_ge(job_done, jobs_through(b, job))
                    nc.vector.tensor_tensor(v_all[:, n, :], misc_ps[:, 0:H], bv_rows[:], ALU.add).then_inc(job_out, 1)
                    return
                dve.wait_ge(hi_done, splits_through(b, job))
                if kind == "x":
                    tok = slice(n * P, (n + 1) * P)
                    src = misc_ps[:, 0:H].rearrange("p (t q) -> p t q", t=FT)
                    nc.vector.tensor_tensor(xt_lo[:, :, tok], src, xt_hi[:, :, tok], ALU.subtract).then_inc(job_out, 1)
                    return
                width, stack, cols, heads = job_parts(job)
                for head, rows, other in heads:
                    last = nc.vector.scalar_tensor_tensor(
                        out=stack[other, head, cols], in0=job_bank(job)[rows, 0:width],
                        scalar=bias_qk[rows, 1 if kind == "k" else 0, n:n + 1], in1=stack[rows, head, cols],
                        op0=ALU.add, op1=ALU.subtract)
                last.then_inc(job_out, 1)

            def body(b, with_next):
                for step in batch_steps(UNITS, with_next):
                    kind = step[0]
                    if kind == "scores":
                        t = step[1]
                        qt = t % 4 // 2
                        dve.wait_ge(scores_done, b * UNITS + (t + 1))
                        dve.wait_ge(turned[1], b * UNITS + (t + 1))
                        if t % 12 in (0, 2):
                            dve.wait_ge(mask_done, b * TT + (2 * (t // 12) + qt + 1))
                        dve.sem_inc(dve_waited, 1)
                        nc.vector.tensor_tensor_reduce(prob[:, t % 3, :], score_ps[:, t % 2, :], mask[:, qt, :],
                                                       1.0, HUGE, ALU.add, ALU.min,
                                                       row_min[:, t % 4:t % 4 + 1]).then_inc(masked, 1)
                    elif kind == "turn":
                        u = step[1]
                        pair, head, qt = u // 4, u % 2, u % 4 // 2
                        if u % 4 == 0:
                            dve.wait_ge(mixed, b * PAIRS + (pair + 1))
                        dve.wait_ge(turned[1], b * UNITS + (u + 4))
                        nc.vector.tensor_copy(prob_t[:, pair % 2, head, 4:8, qt * P:(qt + 1) * P],
                                              turn_ps[:, 1]).then_inc(copied[1], 1)
                    elif kind == "denominators":
                        pair = step[1]
                        dve.wait_ge(exp_done, b * UNITS + 4 * (pair + 1))
                        nc.vector.reciprocal(inv_sum[:, pair % 2, :], row_sum[:, pair % 2, :]).then_inc(inv_done, 1)
                    elif kind == "context":
                        pair = step[1]
                        dve.wait_ge(mixed, b * PAIRS + (pair + 3))
                        dve.wait_ge(spread_in[pair % 2], b * (16 * PAIRS) + 32 * (pair // 2 + 1))
                        dve.wait_ge(context_lo_done, b * PAIRS + (pair + 1))
                        nc.vector.tensor_tensor(context[:], context_ps[:, 0:GQ], inv_rows[:, pair % 2, :],
                                                ALU.mult).then_inc(context_done, 1)
                    elif kind == "job":
                        job_result(b, step[1])
                    elif kind == "project":
                        group, tile = step[1:]
                        n = 2 * group + tile
                        dve.wait_ge(projected, b * TT + (n + 2))
                        dve.wait_ge(res_done, b * TT + (n + 1))
                        nc.vector.tensor_tensor(res[:, n, :], misc_ps[:, 0:H], res[:, n, :],
                                                ALU.add).then_inc(sum_done, 1)
                        dve.wait_ge(sum_done, b * TT + (n + 2))
                        nc.vector.bn_stats(stats[:, tile, :], res[:, n, :]).then_inc(stats_done, 1)
                        dve.wait_ge(stats_done, b * TT + (n + 1))
                        dve.sem_inc(dve_waited, 1)
                        nc.vector.bn_aggr(mean_var[:, tile, :], stats[:, tile, :]).then_inc(mean_done, 1)
                        if tile == 1:
                            dve.wait_ge(mean_done, b * TT + (n + 1))
                            nc.vector.tensor_scalar(var_eps[:], mean_var[:, :, 1], EPS, None,
                                                    ALU.add).then_inc(var_done, 1)
                    elif kind == "normalise":
                        group = step[1]
                        dve.wait_ge(deviation_done, b * 4 + (group + 1))
                        nc.vector.reciprocal(inv_dev[:], deviation[:]).then_inc(inv_dev_done, 1)
                        dve.wait_ge(inv_dev_done, b * 4 + (group + 1))
                        for tile in range(2):
                            n = 2 * group + tile
                            nc.vector.tensor_scalar(res[:, n, :], res[:, n, :], mean_var[:, tile, 0:1],
                                                    inv_dev[:, tile:tile + 1], ALU.subtract,
                                                    ALU.mult).then_inc(normalised, 1)

            dve.wait_ge(biases_in, 64)
            nc.vector.tensor_scalar(bias_qk[:, 0, :], bias_raw[:, 0, :], SCALE, None, ALU.mult).then_inc(bias_scaled, 1)
            nc.vector.tensor_copy(bias_qk[:, 1, :], bias_raw[:, 1, :]).then_inc(bias_scaled, 1)
            for n, w in enumerate((1, 0, 2, 3)):
                dve.wait_ge(weights_hi_done, n + 1)
                nc.vector.scalar_tensor_tensor(out=weight_lo[:, w], in0=weight_raw[:, w],
                                               scalar=SCALE if w == 0 else 1.0, in1=weight_hi[:, w],
                                               op0=ALU.mult, op1=ALU.subtract).then_inc(weights_done, 1)
            dve.wait_ge(bias_scaled, 2)
            for job in start_jobs:
                job_result(None, job)
            with dve.Fori(0, BATCH - 1) as b:
                body(b, True)
            body(BATCH - 1, False)

        @block.gpsimd
        def _(pool):
            pool.sem_inc(context_lo_done, 1)

            def make_mask(qt):
                nc.gpsimd.tensor_scalar(mask[:, qt, :], adj_in[:, qt, :], -NEG, NEG, ALU.mult,
                                        ALU.add).then_inc(mask_done, 1)

            def body(b, with_next):
                for step in batch_steps(UNITS, with_next):
                    kind = step[0]
                    if kind == "mask":
                        group, qt = step[1:]
                        pool.wait_ge(adj_loaded[qt], b * 64 + 16 * (group + 1))
                        pool.wait_ge(masked, b * UNITS + (12 * (group - 1) + 12 + 2 * qt))
                        pool.sem_inc(pool_waited, 1)
                        make_mask(qt)
                    elif kind == "residual":
                        g = step[1]
                        pool.wait_ge(x_loaded[g], b * 16 + 16)
                        pool.wait_ge(stored[g], b * 16 + 16)
                        for n in (2 * g, 2 * g + 1):
                            nc.gpsimd.tensor_tensor(res[:, n, :], x_in[:, n, :], bf_rows[:],
                                                    ALU.add).then_inc(res_done, 1)
                    elif kind == "context":
                        pair = step[1]
                        pool.wait_ge(context_hi_done, b * PAIRS + (pair + 1))
                        nc.gpsimd.tensor_tensor(context_lo[:, pair % 3, :], context[:], context_hi[:, pair % 3, :],
                                                ALU.subtract).then_inc(context_lo_done, 1)

            nc.gpsimd.memset(ident[:], 0.0).then_inc(ident_clear, 1)
            pool.wait_ge(ident_clear, 1)
            nc.gpsimd.affine_select(out=ident[:], in_=ident[:], compare_op=ALU.not_equal, fill=1.0, base=0,
                                    pattern=[[-1, P]], channel_multiplier=1).then_inc(ident_done, 1)
            for qt in range(2):
                pool.wait_ge(adj_loaded[qt], 16)
                make_mask(qt)
            pool.wait_ge(biases_in, 64)
            with pool.Fori(0, BATCH - 1) as b:
                body(b, True)
            body(BATCH - 1, False)


_INS = ["x", "adj", "L0_gnn_Wq", "L0_gnn_bq", "L0_gnn_Wk", "L0_gnn_bk", "L0_gnn_Wv", "L0_gnn_bv", "L0_gnn_Wf",
        "L0_gnn_bf"]


def kernel(**inputs):
    import numpy as _np
    import concourse.bacc as _bacc
    from concourse.bass_utils import run_bass_kernel_spmd as _run

    nc = _bacc.Bacc("TRN2", target_bir_lowering=False, num_devices=1)
    arrays, args = {}, []
    for name in _INS:
        a = _np.ascontiguousarray(inputs[name])
        arrays[f"in_{name}_dram"] = a
        args.append(nc.dram_tensor(f"in_{name}_dram", a.shape, mybir.dt.from_np(a.dtype), kind="ExternalInput").ap())
    out = nc.dram_tensor("out_0_dram", inputs["x"].shape, F32, kind="ExternalOutput").ap()
    graph_attention(nc, *args, out)
    return _run(nc, [arrays], core_ids=[0]).results[0]["out_0_dram"]
```

```python
from contextlib import ExitStack

import concourse.bass as bass
from concourse import mybir

F32 = mybir.dt.float32
F32R = mybir.dt.float32r
I32 = mybir.dt.int32
U8 = mybir.dt.uint8
ALU = mybir.AluOpType
ACT = mybir.ActivationFunctionType

P = 128
NEG = 9.0e15
EPS = 1e-5
HUGE = 3.0e38
HEADS = 6
ROOT_MAGIC = 0x5F3759DF
NEWTON_STEPS = 3
ROOT_OPS = 4 * NEWTON_STEPS


def first_jobs():
    return [("k", 0, 0), ("k", 0, 1), ("q", 0, 0), ("k", 1, 0), ("q", 1, 0), ("k", 1, 1), ("k", 2, 0), ("k", 2, 1),
            ("q", 2, 0)]


def start_steps():
    x_jobs = [("job", ("x", n, 0)) for n in range(8)]
    jobs = [("job", job) for job in first_jobs()]
    return [("weight", 1)] + x_jobs + [("weight", 0), ("weight", 2)] + jobs[:1] + [("weight", 3)] + jobs[1:]


def batch_steps(units, with_next):
    steps = []
    q_steps = (8, 10, 14, 18, 24, 26, 30, 36, 38)
    x_steps = (39, 40, 41, 42, 43, 45, 47)
    for t in range(units):
        if t == 0:
            steps.append(("job", ("v", 0, 0)))
        steps.append(("scores", t))
        if 1 <= t < 8:
            steps.append(("job", ("v", t, 0)))
        elif t in q_steps:
            n = q_steps.index(t)
            steps.append(("job", ("q", n % 3, 1 + n // 3)))
        elif t >= 20 and (t - 20) % 12 in (0, 2):
            steps.append(("project", (t - 20) // 12, (t - 20) % 12 // 2))
        elif t in x_steps and with_next:
            steps.append(("job", ("x", x_steps.index(t), 0)))
        if t >= 7 and t % 2 == 1:
            steps.append(("mix", (t - 7) // 4, (t - 7) % 4 // 2))
        if t >= 2:
            steps.append(("turn", t - 2))
        steps.append(("exp", t))
        if t % 4 == 1 and t >= 5:
            steps.append(("denominators", (t - 5) // 4))
        if t % 4 == 2 and t >= 6:
            steps.append(("spread", (t - 6) // 4))
        if t % 4 == 1 and t >= 9:
            steps.append(("context", (t - 9) // 4))
        if t >= 24 and t % 12 == 0:
            steps.append(("normalise", (t - 24) // 12))
        if t >= 27 and (t - 27) % 12 == 0:
            steps.append(("store", (t - 27) // 12))
        if 8 <= t < 12:
            steps.append(("residual", t - 8))
        if t == 12 and with_next:
            steps.append(("load x",))
        if t % 12 >= 10 and (t < 40 or with_next):
            steps.append(("mask", t // 12 + 1, t % 12 - 10))
    jobs = [("job", j) for j in first_jobs()] if with_next else []
    last = units // 4 - 1
    steps += [("job", ("x", 7, 0))] if with_next else []
    steps += [("turn", units - 2), ("mix", last - 1, 1), ("turn", units - 1), ("denominators", last)]
    steps += [("context", last - 1), ("normalise", 2)] + jobs[:2]
    steps += [("spread", last), ("store", 2), ("mix", last, 0), ("mix", last, 1), ("context", last)] + jobs[2:5]
    steps += [("project", 3, 0)] + jobs[5:6] + [("project", 3, 1)] + jobs[6:7]
    steps += [("normalise", 3)] + jobs[7:] + [("store", 3)]
    return steps


def graph_attention(nc, x, adj, wq, bq, wk, bk, wv, bv, wf, bf, out):
    BATCH, S, H = x.shape
    FT = H // P
    TT = S // P
    HS = H // HEADS
    GQ = 2 * P
    UNITS = HEADS * TT
    PAIRS = UNITS // 4
    assert (S, H, HS, FT) == (1024, 384, 64, 3)
    SCALE = -1.0 / 8.0

    first = first_jobs()
    start_jobs = [("x", n, 0) for n in range(TT)] + first
    loop_jobs = [("v", n, 0) for n in range(TT)] + [("q", n % 3, 1 + n // 3) for n in range(9)] + start_jobs
    loop_splits = [j for j in loop_jobs if j[0] != "v"]

    x_tiles = x.rearrange("b (t p) h -> b p t h", p=P)
    out_tiles = out.rearrange("b (t p) h -> b p t h", p=P)
    adj_rows = adj.rearrange("b s k -> (b s) k")
    spread_dram = nc.dram_tensor("spread_dram", [2, 4, P], F32, kind="Internal").ap()

    with ExitStack() as ctx:
        def sb(name, shape, dt):
            return ctx.enter_context(nc.sbuf_tensor(name, shape, dt))

        def sem(name):
            return ctx.enter_context(nc.semaphore(name))

        k_stack = sb("k_stack", [P, HEADS, S], F32R)
        q_home = sb("q_home", [P, HEADS, GQ], F32R)
        q_swap = sb("q_swap", [P, HEADS, GQ], F32R)
        v_all = sb("v_all", [P, TT, H], F32)
        xt_hi = sb("xt_hi", [P, FT, S], F32R)
        xt_lo = sb("xt_lo", [P, FT, S], F32R)
        weight_hi = sb("weight_hi", [P, 4, FT, H], F32R)
        weight_lo = sb("weight_lo", [P, 4, FT, H], F32R)
        x_in = sb("x_in", [P, TT, H], F32)
        res = sb("res", [P, TT, H], F32)
        adj_in = sb("adj_in", [P, 2, S], U8)
        mask = sb("mask", [P, 2, S], F32)
        prob = sb("prob", [P, 3, S], F32)
        prob_t = sb("prob_t", [P, 2, 2, TT, GQ], F32)
        context = sb("context", [P, GQ], F32)
        context_hi = sb("context_hi", [P, FT, GQ], F32R)
        context_lo = sb("context_lo", [P, FT, GQ], F32R)
        inv_rows = sb("inv_rows", [P, 2, GQ], F32)
        ident = sb("ident", [P, P], F32)
        bias_raw = sb("bias_raw", [P, 2, FT], F32)
        bias_qk = sb("bias_qk", [P, 2, FT], F32)
        bv_rows = sb("bv_rows", [P, H], F32)
        bf_rows = sb("bf_rows", [P, H], F32)
        row_min = sb("row_min", [P, 4], F32)
        row_sum = sb("row_sum", [P, 2, 4], F32)
        inv_sum = sb("inv_sum", [P, 2, 4], F32)
        stats = sb("stats", [P, 2, 6], F32)
        mean_var = sb("mean_var", [P, 2, 2], F32)
        var_eps = sb("var_eps", [P, 2], F32)
        newton = sb("newton", [P, 2], F32)
        inv_dev = sb("inv_dev", [P, 2], F32)

        score_ps = ctx.enter_context(nc.psum_tensor("score_ps", [P, 2, S], F32))
        turn_ps = ctx.enter_context(nc.psum_tensor("turn_ps", [P, 2, 4, P], F32))
        context_ps = ctx.enter_context(nc.psum_tensor("context_ps", [P, 512], F32))
        misc_ps = ctx.enter_context(nc.psum_tensor("misc_ps", [P, 512], F32))
        weight_raw = prob_t[:].rearrange("p a b c d -> p (a b c d)")[:, 0:4 * FT * H].rearrange(
            "p (w t h) -> p w t h", w=4, t=FT)

        weights_in = [sem(f"weights_in{w}") for w in range(4)]
        qk_biases_in = sem("qk_biases_in")
        vf_biases_in = sem("vf_biases_in")
        bias_scaled = sem("bias_scaled")
        weights_hi_done = sem("weights_hi_done")
        weights_done = sem("weights_done")
        ident_clear = sem("ident_clear")
        ident_done = sem("ident_done")
        x_loaded = [sem(f"x_loaded{g}") for g in range(4)]
        adj_loaded = [sem(f"adj_loaded{i}") for i in range(2)]
        mask_done = sem("mask_done")
        scores_done = sem("scores_done")
        masked = sem("masked")
        exp_done = sem("exp_done")
        turned = [sem(f"turned{i}") for i in range(2)]
        copied = [sem(f"copied{i}") for i in range(2)]
        mixed = sem("mixed")
        inv_done = sem("inv_done")
        spread_out = [sem(f"spread_out{i}") for i in range(2)]
        spread_in = [sem(f"spread_in{i}") for i in range(2)]
        context_done = sem("context_done")
        context_hi_done = sem("context_hi_done")
        context_lo_done = sem("context_lo_done")
        job_done = sem("job_done")
        hi_done = sem("hi_done")
        job_out = sem("job_out")
        q_swapped = [sem(f"q_swapped{pair}") for pair in range(3)]
        projected = sem("projected")
        res_done = sem("res_done")
        sum_done = sem("sum_done")
        stats_done = sem("stats_done")
        mean_done = sem("mean_done")
        var_done = sem("var_done")
        guess_done = sem("guess_done")
        root_ops = sem("root_ops")
        normalised = sem("normalised")
        dve_waited = sem("dve_waited")
        pool_waited = sem("pool_waited")
        stored = [sem(f"stored{g}") for g in range(4)]

        def jobs_through(b, job, before=start_jobs, loop=loop_jobs):
            if b is None:
                return before.index(job) + 1
            return b * len(loop) + (len(before) + loop.index(job) + 1)

        def splits_through(b, job):
            return jobs_through(b, job, start_jobs, loop_splits)

        def first_jobs_through(b, job):
            return b * len(loop_jobs) + (start_jobs.index(job) + 1)

        def score_bank(job):
            return (first.index(job) + 3) % 4

        def job_bank(b, job):
            if job in first or b is None:
                bank = score_bank(job) if job in first else job[1] % 4
                return score_ps[:, bank // 2, (bank % 2) * 512:(bank % 2) * 512 + 512]
            return misc_ps[:]

        def job_parts(job):
            kind, pair, piece = job
            if kind == "k":
                width, cols, stack = 512, slice(piece * 512, piece * 512 + 512), k_stack
            else:
                width, cols, stack = GQ, slice(0, GQ), q_home
            upper, lower = slice(0, 64), slice(64, P)
            return width, stack, cols, ((2 * pair, upper, lower), (2 * pair + 1, lower, upper))

        def vector_normalises(group, with_next):
            return group == 2 or not with_next

        def scale_rows(engine, group):
            for tile in range(2):
                n = 2 * group + tile
                engine.tensor_scalar(res[:, n, :], res[:, n, :], mean_var[:, tile, 0:1], inv_dev[:, tile:tile + 1],
                                     ALU.subtract, ALU.mult).then_inc(normalised, 1)

        block = ctx.enter_context(nc.Block())

        @block.sync
        def _(sp):
            def load_x(b):
                for g in range(4):
                    sp.dma_start(x_in[:, 2 * g:2 * g + 2, :], x_tiles[b, :, 2 * g:2 * g + 2, :]
                                 ).then_inc(x_loaded[g], 16)

            def load_weight(w, src):
                sp.dma_start(weight_raw[:, w], src.rearrange("(t p) n -> p t n", p=P)).then_inc(weights_in[w], 16)

            load_weight(1, wk)
            load_x(0)
            load_weight(0, wq)
            for n, bias in enumerate((bq, bk)):
                sp.dma_start(bias_raw[:, n, :], bias.rearrange("(t p) -> p t", p=P),
                             allow_slow_non_contiguous=True).then_inc(qk_biases_in, 16)
            load_weight(2, wv)
            load_weight(3, wf)
            sp.dma_start(bv_rows[:], bv.partition_broadcast(P)).then_inc(vf_biases_in, 16)
            sp.dma_start(bf_rows[:], bf.partition_broadcast(P)).then_inc(vf_biases_in, 16)
            for qt in range(2):
                sp.dma_start(adj_in[:, qt, :], adj_rows[qt * P:(qt + 1) * P, :]).then_inc(adj_loaded[qt], 16)
            for g in range(4):
                sp.sem_inc(stored[g], 16)

            def swap_q(b, job):
                pair = job[1]
                sp.wait_ge(job_out, jobs_through(b, job))
                for to, at in ((0, 64), (64, 0)):
                    sp.dma_start(q_swap[to:to + 64, 2 * pair:2 * pair + 2, :].bitcast(F32),
                                 q_home[at:at + 64, 2 * pair:2 * pair + 2, :].bitcast(F32)
                                 ).then_inc(q_swapped[pair], 16)

            def body(b, with_next):
                for step in batch_steps(UNITS, with_next):
                    kind = step[0]
                    if kind == "job" and step[1][0] == "q":
                        swap_q(b, step[1])
                    elif kind == "denominators":
                        pair = step[1]
                        sp.wait_ge(inv_done, b * PAIRS + (pair + 1))
                        sp.wait_ge(context_done, b * PAIRS + (pair + 1))
                        sp.dma_start(spread_dram[pair % 2].rearrange("c p -> p c"), inv_sum[:, pair % 2, :],
                                     allow_slow_non_contiguous=True).then_inc(spread_out[pair % 2], 16)
                    elif kind == "spread":
                        pair = step[1]
                        sp.wait_ge(spread_out[pair % 2], b * (8 * PAIRS) + 16 * (pair // 2 + 1))
                        for head in range(2):
                            src = spread_dram[pair % 2, 2 * head:2 * head + 2, :].rearrange("c p -> (c p)")
                            sp.dma_start(inv_rows[64 * head:64 * head + 64, pair % 2, :],
                                         src.partition_broadcast(64)).then_inc(spread_in[pair % 2], 16)
                    elif kind == "mask":
                        group, qt = step[1:]
                        if not with_next and group == 3:
                            continue
                        sp.wait_ge(mask_done, b * 8 + (2 * group + qt + 1))
                        sp.dma_start(adj_in[:, qt, :],
                                     adj_rows[bass.ds(b * S + ((group + 1) * GQ + qt * P), P), :]
                                     ).then_inc(adj_loaded[qt], 16)
                    elif kind == "load x":
                        sp.wait_ge(res_done, b * TT + TT)
                        load_x(b + 1)
                    elif kind == "store":
                        group = step[1]
                        sp.wait_ge(normalised, b * TT + 2 * (group + 1))
                        sp.dma_start(out_tiles[b, :, 2 * group:2 * group + 2, :],
                                     res[:, 2 * group:2 * group + 2, :]).then_inc(stored[group], 16)

            for pair in range(2):
                swap_q(None, ("q", pair, 0))
            sp.wait_ge(mask_done, 2)
            for qt in range(2):
                sp.dma_start(adj_in[:, qt, :],
                             adj_rows[GQ + qt * P:GQ + (qt + 1) * P, :]).then_inc(adj_loaded[qt], 16)
            swap_q(None, ("q", 2, 0))
            with sp.Fori(0, BATCH - 1) as b:
                body(b, True)
            body(BATCH - 1, False)
            for g in range(4):
                sp.wait_ge(stored[g], 16 * (BATCH + 1))

        @block.tensor
        def _(pe):
            pe.sem_inc(turned[1], 3)
            pe.sem_inc(mixed, 2)
            pe.sem_inc(projected, 1)

            def three_products(dst, pieces):
                for t, (left_hi, left_lo, right_hi, right_lo) in enumerate(pieces):
                    pe.matmul(dst, left_hi, right_hi, start=(t == 0), stop=False)
                    pe.matmul(dst, left_hi, right_lo, start=False, stop=False)
                    last = pe.matmul(dst, left_lo, right_hi, start=False, stop=(t == FT - 1))
                return last

            def wait_misc(b, last_job, sums):
                pe.wait_ge(job_out, last_job)
                pe.wait_ge(sum_done, b * TT + (sums + 1))

            def transpose_x(b, tile, last_job, sums):
                if tile % 2 == 0:
                    pe.wait_ge(x_loaded[tile // 2], 16 if b is None else b * 16 + 32)
                if b is not None:
                    wait_misc(b, last_job, sums)
                elif tile >= 4:
                    pe.wait_ge(job_out, tile - 3)
                bank = job_bank(b, ("x", tile, 0))
                for t in range(FT):
                    last = pe.transpose(bank[:, t * P:(t + 1) * P], x_in[:, tile, t * P:(t + 1) * P], ident[:])
                last.then_inc(job_done, 1)

            def wait_score_bank(b, job):
                k = first.index(job)
                if k == 0:
                    pe.wait_ge(job_out, jobs_through(b, ("x", TT - 1, 0)))
                if k >= 4:
                    pe.wait_ge(job_out, jobs_through(b, first[k - 4]))
                elif b is not None:
                    pe.wait_ge(masked, b * UNITS + (UNITS + 1 + score_bank(job) // 2))

            def project_qk(b, kind, pair, piece):
                w, width = (1, 512) if kind == "k" else (0, GQ)
                feat = slice(pair * P, (pair + 1) * P)
                tok = slice(piece * width, (piece + 1) * width)
                three_products(job_bank(b, (kind, pair, piece))[:, 0:width], [
                    (weight_hi[:, w, t, feat], weight_lo[:, w, t, feat], xt_hi[:, t, tok], xt_lo[:, t, tok])
                    for t in range(FT)]).then_inc(job_done, 1)

            def project_v(tile):
                tok = slice(tile * P, (tile + 1) * P)
                three_products(misc_ps[:, 0:H], [
                    (xt_hi[:, t, tok], xt_lo[:, t, tok], weight_hi[:, 2, t, :], weight_lo[:, 2, t, :])
                    for t in range(FT)]).then_inc(job_done, 1)

            def body(b, with_next):
                sums = 0
                misc_job = first_jobs_through(b, ("x", TT - 1, 0))
                for step in batch_steps(UNITS, with_next):
                    kind = step[0]
                    if kind == "scores":
                        t = step[1]
                        group, pair, head, qt = t // 12, t % 12 // 4, t % 2, t % 4 // 2
                        h = 2 * pair + head
                        pe.wait_ge(masked, b * UNITS + (t + 1))
                        if t < 2:
                            pe.wait_ge(job_out, first_jobs_through(b, first[6 + 2 * t]))
                        if t % 4 == 0:
                            pe.wait_ge(q_swapped[pair], b * 128 + 32 * (group + 1))
                        q = slice(qt * P, (qt + 1) * P)
                        for n, q_stack in enumerate((q_home, q_swap)):
                            for half in range(2):
                                keys = slice(half * 512, half * 512 + 512)
                                last = pe.matmul(score_ps[:, t % 2, keys], q_stack[:, h, q], k_stack[:, h, keys],
                                                 start=(n == 0), stop=(n == 1))
                        last.then_inc(scores_done, 1)
                    elif kind == "turn":
                        u = step[1]
                        pe.wait_ge(exp_done, b * UNITS + (u + 1))
                        for half in range(2):
                            pe.wait_ge(copied[half], b * UNITS + (u + 1))
                            for i in range(4):
                                kt = 4 * half + i
                                last = pe.transpose(turn_ps[:, half, i, :], prob[:, u % 3, kt * P:(kt + 1) * P],
                                                    ident[:])
                            last.then_inc(turned[half], 1)
                    elif kind == "mix":
                        pair, chunk = step[1:]
                        if chunk == 0:
                            for half in range(2):
                                pe.wait_ge(copied[half], b * UNITS + (4 * pair + 5))
                            pe.wait_ge(context_done, b * PAIRS + (pair + 2))
                        if pair == 0:
                            pe.wait_ge(job_out, jobs_through(b, ("v", 4 * chunk + 3, 0)))
                        for kt in range(4 * chunk, 4 * chunk + 4):
                            for head in range(2):
                                col = (2 * (pair % 3) + head) * HS
                                last = pe.matmul(context_ps[64 * head:64 * head + 64, 0:GQ],
                                                 v_all[:, kt, col:col + HS], prob_t[:, pair % 2, head, kt, :],
                                                 start=(kt == 0), stop=(kt == TT - 1))
                        if chunk == 1:
                            last.then_inc(mixed, 1)
                    elif kind == "job":
                        job = step[1]
                        if job[0] == "x":
                            transpose_x(b, job[1], misc_job, sums)
                            misc_job = jobs_through(b, job)
                        elif job in first:
                            wait_score_bank(b, job)
                            project_qk(b, *job)
                        else:
                            wait_misc(b, misc_job, sums)
                            if job[0] == "v":
                                project_v(job[1])
                            else:
                                project_qk(b, *job)
                            misc_job = jobs_through(b, job)
                    elif kind == "project":
                        group, tile = step[1:]
                        wait_misc(b, misc_job, sums)
                        if tile == 0:
                            pe.wait_ge(context_lo_done, b * PAIRS + (3 * group + 4))
                        tok = slice(tile * P, (tile + 1) * P)
                        three_products(misc_ps[:, 0:H], [
                            (context_hi[:, t, tok], context_lo[:, t, tok], weight_hi[:, 3, t, :],
                             weight_lo[:, 3, t, :]) for t in range(FT)]).then_inc(projected, 1)
                        sums += 1

            pe.wait_ge(ident_done, 1)
            for tile in range(TT):
                transpose_x(None, tile, None, 0)
            for job in first:
                pe.wait_ge(weights_done, 1 if job[0] == "k" else 2)
                wait_score_bank(None, job)
                project_qk(None, *job)
            pe.wait_ge(weights_done, 4)
            with pe.Fori(0, BATCH - 1) as b:
                body(b, True)
            body(BATCH - 1, False)

        @block.scalar
        def _(act):
            act.sem_inc(copied[0], 1)

            def high_part(b, job):
                kind, n, piece = job
                act.wait_ge(job_done, jobs_through(b, job))
                if kind == "x":
                    src = job_bank(b, job)[:, 0:H].rearrange("p (t q) -> p t q", t=FT)
                    nc.scalar.activation(xt_hi[:, :, n * P:(n + 1) * P], src, ACT.Copy).then_inc(hi_done, 1)
                    return
                width, stack, cols, heads = job_parts(job)
                for head, rows, _ in heads:
                    last = nc.scalar.activation(stack[rows, head, cols], job_bank(b, job)[rows, 0:width], ACT.Identity,
                                                bias=bias_qk[rows, 1 if kind == "k" else 0, n:n + 1])
                last.then_inc(hi_done, 1)

            def body(b, with_next):
                for step in batch_steps(UNITS, with_next):
                    kind = step[0]
                    if kind == "turn":
                        u = step[1]
                        pair, head, qt = u // 4, u % 2, u % 4 // 2
                        if u % 4 == 0:
                            act.wait_ge(mixed, b * PAIRS + (pair + 1))
                        act.wait_ge(turned[0], b * UNITS + (u + 1))
                        nc.scalar.activation(prob_t[:, pair % 2, head, 0:4, qt * P:(qt + 1) * P],
                                             turn_ps[:, 0], ACT.Copy).then_inc(copied[0], 1)
                    elif kind == "exp":
                        t = step[1]
                        col = 2 * (t % 2) + t % 4 // 2
                        act.wait_ge(masked, b * UNITS + (t + 3))
                        nc.scalar.activation(prob[:, t % 3, :], prob[:, t % 3, :], ACT.Exp, scale=-1.0,
                                             bias=row_min[:, t % 4:t % 4 + 1],
                                             accum_out=row_sum[:, t // 4 % 2, col:col + 1]).then_inc(exp_done, 1)
                    elif kind == "job" and step[1][0] != "v":
                        high_part(b, step[1])
                    elif kind == "context":
                        pair = step[1]
                        act.wait_ge(context_done, b * PAIRS + (pair + 3))
                        if pair % 3 == 0:
                            act.wait_ge(projected, b * TT + (2 * (pair // 3) + 1))
                        nc.scalar.activation(context_hi[:, pair % 3, :], context[:],
                                             ACT.Copy).then_inc(context_hi_done, 1)

            for kind, what in start_steps():
                if kind == "weight":
                    act.wait_ge(weights_in[what], 16)
                    nc.scalar.activation(weight_hi[:, what], weight_raw[:, what], ACT.Copy,
                                         scale=SCALE if what == 0 else 1.0).then_inc(weights_hi_done, 1)
                else:
                    if what == first[0]:
                        act.wait_ge(bias_scaled, 2)
                    high_part(None, what)
            with act.Fori(0, BATCH - 1) as b:
                body(b, True)
            body(BATCH - 1, False)

        @block.vector
        def _(dve):
            dve.sem_inc(masked, 2)
            dve.sem_inc(copied[1], 1)
            dve.sem_inc(context_done, 2)
            dve.sem_inc(sum_done, 1)

            def job_result(b, job):
                kind, n, piece = job
                if kind == "v":
                    dve.wait_ge(job_done, jobs_through(b, job))
                    nc.vector.tensor_tensor(v_all[:, n, :], misc_ps[:, 0:H], bv_rows[:], ALU.add).then_inc(job_out, 1)
                    return
                dve.wait_ge(hi_done, splits_through(b, job))
                if kind == "x":
                    tok = slice(n * P, (n + 1) * P)
                    src = job_bank(b, job)[:, 0:H].rearrange("p (t q) -> p t q", t=FT)
                    nc.vector.tensor_tensor(xt_lo[:, :, tok], src, xt_hi[:, :, tok], ALU.subtract).then_inc(job_out, 1)
                    return
                width, stack, cols, heads = job_parts(job)
                for head, rows, other in heads:
                    last = nc.vector.scalar_tensor_tensor(
                        out=stack[other, head, cols], in0=job_bank(b, job)[rows, 0:width],
                        scalar=bias_qk[rows, 1 if kind == "k" else 0, n:n + 1], in1=stack[rows, head, cols],
                        op0=ALU.add, op1=ALU.subtract)
                last.then_inc(job_out, 1)

            def body(b, with_next):
                for step in batch_steps(UNITS, with_next):
                    kind = step[0]
                    if kind == "scores":
                        t = step[1]
                        qt = t % 4 // 2
                        dve.wait_ge(scores_done, b * UNITS + (t + 1))
                        dve.wait_ge(turned[1], b * UNITS + (t + 1))
                        if t % 12 in (0, 2):
                            dve.wait_ge(mask_done, b * TT + (2 * (t // 12) + qt + 1))
                        dve.sem_inc(dve_waited, 1)
                        nc.vector.tensor_tensor_reduce(prob[:, t % 3, :], score_ps[:, t % 2, :], mask[:, qt, :],
                                                       1.0, HUGE, ALU.add, ALU.min,
                                                       row_min[:, t % 4:t % 4 + 1]).then_inc(masked, 1)
                    elif kind == "turn":
                        u = step[1]
                        pair, head, qt = u // 4, u % 2, u % 4 // 2
                        if u % 4 == 0:
                            dve.wait_ge(mixed, b * PAIRS + (pair + 1))
                        dve.wait_ge(turned[1], b * UNITS + (u + 4))
                        nc.vector.tensor_copy(prob_t[:, pair % 2, head, 4:8, qt * P:(qt + 1) * P],
                                              turn_ps[:, 1]).then_inc(copied[1], 1)
                    elif kind == "denominators":
                        pair = step[1]
                        dve.wait_ge(exp_done, b * UNITS + 4 * (pair + 1))
                        nc.vector.reciprocal(inv_sum[:, pair % 2, :], row_sum[:, pair % 2, :]).then_inc(inv_done, 1)
                    elif kind == "context":
                        pair = step[1]
                        dve.wait_ge(mixed, b * PAIRS + (pair + 3))
                        dve.wait_ge(spread_in[pair % 2], b * (16 * PAIRS) + 32 * (pair // 2 + 1))
                        dve.wait_ge(context_lo_done, b * PAIRS + (pair + 1))
                        nc.vector.tensor_tensor(context[:], context_ps[:, 0:GQ], inv_rows[:, pair % 2, :],
                                                ALU.mult).then_inc(context_done, 1)
                    elif kind == "job":
                        job_result(b, step[1])
                    elif kind == "project":
                        group, tile = step[1:]
                        n = 2 * group + tile
                        dve.wait_ge(projected, b * TT + (n + 2))
                        dve.wait_ge(res_done, b * TT + (n + 1))
                        nc.vector.tensor_tensor(res[:, n, :], misc_ps[:, 0:H], res[:, n, :],
                                                ALU.add).then_inc(sum_done, 1)
                        dve.wait_ge(sum_done, b * TT + (n + 2))
                        nc.vector.bn_stats(stats[:, tile, :], res[:, n, :]).then_inc(stats_done, 1)
                        dve.wait_ge(stats_done, b * TT + (n + 1))
                        dve.sem_inc(dve_waited, 1)
                        nc.vector.bn_aggr(mean_var[:, tile, :], stats[:, tile, :]).then_inc(mean_done, 1)
                        if tile == 1:
                            dve.wait_ge(mean_done, b * TT + (n + 1))
                            nc.vector.tensor_scalar(var_eps[:], mean_var[:, :, 1], EPS, None,
                                                    ALU.add).then_inc(var_done, 1)
                            dve.wait_ge(var_done, b * 4 + (group + 1))
                            nc.vector.tensor_scalar(inv_dev[:].bitcast(I32), var_eps[:].bitcast(I32), -0.5,
                                                    float(ROOT_MAGIC), ALU.mult, ALU.add).then_inc(guess_done, 1)
                    elif kind == "normalise" and vector_normalises(step[1], with_next):
                        group = step[1]
                        dve.wait_ge(root_ops, (b * 4 + group + 1) * ROOT_OPS)
                        scale_rows(nc.vector, group)

            weights = 0
            for kind, what in start_steps():
                if kind == "weight":
                    weights += 1
                    dve.wait_ge(weights_hi_done, weights)
                    nc.vector.scalar_tensor_tensor(out=weight_lo[:, what], in0=weight_raw[:, what],
                                                   scalar=SCALE if what == 0 else 1.0, in1=weight_hi[:, what],
                                                   op0=ALU.mult, op1=ALU.subtract).then_inc(weights_done, 1)
                    continue
                if what == first[0]:
                    dve.wait_ge(qk_biases_in, 32)
                    nc.vector.tensor_scalar(bias_qk[:, 0, :], bias_raw[:, 0, :], SCALE, None,
                                            ALU.mult).then_inc(bias_scaled, 1)
                    nc.vector.tensor_copy(bias_qk[:, 1, :], bias_raw[:, 1, :]).then_inc(bias_scaled, 1)
                    dve.wait_ge(bias_scaled, 2)
                job_result(None, what)
            dve.wait_ge(vf_biases_in, 32)
            with dve.Fori(0, BATCH - 1) as b:
                body(b, True)
            body(BATCH - 1, False)

        @block.gpsimd
        def _(pool):
            pool.sem_inc(context_lo_done, 1)

            def make_mask(qt):
                nc.gpsimd.tensor_scalar(mask[:, qt, :], adj_in[:, qt, :], -NEG, NEG, ALU.mult,
                                        ALU.add).then_inc(mask_done, 1)

            def inverse_root(before):
                ops = 0

                def result(instruction):
                    nonlocal ops
                    ops += 1
                    instruction.then_inc(root_ops, 1)
                    pool.wait_ge(root_ops, before + ops)

                for _ in range(NEWTON_STEPS):
                    result(nc.gpsimd.tensor_tensor(newton[:], inv_dev[:], inv_dev[:], ALU.mult))
                    result(nc.gpsimd.tensor_tensor(newton[:], newton[:], var_eps[:], ALU.mult))
                    pool.sem_inc(pool_waited, 1)
                    result(nc.gpsimd.tensor_scalar(newton[:], newton[:], -0.5, 1.5, ALU.mult, ALU.add))
                    result(nc.gpsimd.tensor_tensor(inv_dev[:], inv_dev[:], newton[:], ALU.mult))

            def body(b, with_next):
                for step in batch_steps(UNITS, with_next):
                    kind = step[0]
                    if kind == "mask":
                        group, qt = step[1:]
                        pool.wait_ge(adj_loaded[qt], b * 64 + 16 * (group + 1))
                        pool.wait_ge(masked, b * UNITS + (12 * (group - 1) + 12 + 2 * qt))
                        pool.sem_inc(pool_waited, 1)
                        make_mask(qt)
                    elif kind == "residual":
                        g = step[1]
                        pool.wait_ge(x_loaded[g], b * 16 + 16)
                        pool.wait_ge(stored[g], b * 16 + 16)
                        for n in (2 * g, 2 * g + 1):
                            nc.gpsimd.tensor_tensor(res[:, n, :], x_in[:, n, :], bf_rows[:],
                                                    ALU.add).then_inc(res_done, 1)
                    elif kind == "context":
                        pair = step[1]
                        pool.wait_ge(context_hi_done, b * PAIRS + (pair + 1))
                        nc.gpsimd.tensor_tensor(context_lo[:, pair % 3, :], context[:], context_hi[:, pair % 3, :],
                                                ALU.subtract).then_inc(context_lo_done, 1)
                    elif kind == "normalise":
                        group = step[1]
                        pool.wait_ge(guess_done, b * 4 + (group + 1))
                        inverse_root((b * 4 + group) * ROOT_OPS)
                        if not vector_normalises(group, with_next):
                            pool.sem_inc(pool_waited, 1)
                            scale_rows(nc.gpsimd, group)

            nc.gpsimd.memset(ident[:], 0.0).then_inc(ident_clear, 1)
            pool.wait_ge(ident_clear, 1)
            nc.gpsimd.affine_select(out=ident[:], in_=ident[:], compare_op=ALU.not_equal, fill=1.0, base=0,
                                    pattern=[[-1, P]], channel_multiplier=1).then_inc(ident_done, 1)
            for qt in range(2):
                pool.wait_ge(adj_loaded[qt], 16)
                make_mask(qt)
            pool.wait_ge(vf_biases_in, 32)
            with pool.Fori(0, BATCH - 1) as b:
                body(b, True)
            body(BATCH - 1, False)


_INS = ["x", "adj", "L0_gnn_Wq", "L0_gnn_bq", "L0_gnn_Wk", "L0_gnn_bk", "L0_gnn_Wv", "L0_gnn_bv", "L0_gnn_Wf",
        "L0_gnn_bf"]


def kernel(**inputs):
    import numpy as _np
    import concourse.bacc as _bacc
    from concourse.bass_utils import run_bass_kernel_spmd as _run

    nc = _bacc.Bacc("TRN2", target_bir_lowering=False, num_devices=1)
    arrays, args = {}, []
    for name in _INS:
        a = _np.ascontiguousarray(inputs[name])
        arrays[f"in_{name}_dram"] = a
        args.append(nc.dram_tensor(f"in_{name}_dram", a.shape, mybir.dt.from_np(a.dtype), kind="ExternalInput").ap())
    out = nc.dram_tensor("out_0_dram", inputs["x"].shape, F32, kind="ExternalOutput").ap()
    graph_attention(nc, *args, out)
    return _run(nc, [arrays], core_ids=[0]).results[0]["out_0_dram"]
```
